# Optimizing a Trainium2 kernel written in Bass

```python
import numpy as np
import jax
import jax.numpy as jnp

def _softmax(x, axis=-1):
    return jax.nn.softmax(x, axis=axis)

def _gelu(x):
    return jax.nn.gelu(x, approximate=True)

def _silu(x):
    return jax.nn.silu(x)

def _sigmoid(x):
    return jax.nn.sigmoid(x)

def _layernorm(x, axis=-1, eps=1e-05):
    m = jnp.mean(x, axis=axis, keepdims=True)
    v = jnp.var(x, axis=axis, keepdims=True)
    return (x - m) / jnp.sqrt(v + eps)

def _scatter_add(tgt, idx, src, axis=0):
    return tgt.at[idx].add(src)

def _segment_sum(src, seg, n):
    return jax.ops.segment_sum(src, seg, n)
kernel_name = 'mk_gnn_resnorm_d2_gnn_r16_31dfb3'

def setup_inputs(seed: int=0):
    np.random.seed(seed)
    _w = jnp.asarray

    def _rec_inputs():
        import jax
        import jax.numpy as jnp
        _gk = jax.random.key(seed)
        x = -0.0003713 + 1 * jax.random.normal(jax.random.fold_in(_gk, 1), (6250, 128), jnp.float32)
        src = jax.random.randint(jax.random.fold_in(_gk, 2), (100000,), 0, 6250, jnp.int32)
        dst = jnp.minimum((6250 * jax.random.uniform(jax.random.fold_in(_gk, 3), (100000,)) ** 2.0).astype(jnp.int32), 99999)
        _o = jnp.argsort(dst, stable=True)
        src = src[_o]
        dst = dst[_o]
        return (x, src, dst)
    x, src, dst = _rec_inputs()

    def _L0_gnn_setup():
        import jax, jax.numpy as jnp
        import numpy as np
        N, E = (6250, 100000)
        IN_DIM, HID, OUT_DIM = (128, 256, 128)
        LN_EPS = 1e-05

        def _gcn_norm(edge_index, n_nodes):
            loops = jnp.arange(n_nodes, dtype=edge_index.dtype)
            src = jnp.concatenate([edge_index[0], loops])
            dst = jnp.concatenate([edge_index[1], loops])
            deg = jax.ops.segment_sum(jnp.ones_like(dst, dtype=jnp.float32), dst, num_segments=n_nodes)
            dinv = jnp.where(deg > 0, jax.lax.rsqrt(deg), 0.0)
            norm = dinv[src] * dinv[dst]
            return (src, dst, norm)

        def _gcn_conv(x, W, b, src, dst, norm, n_nodes):
            h = x @ W
            msg = h[src] * norm[:, None]
            out = jax.ops.segment_sum(msg, dst, num_segments=n_nodes)
            return out + b

        def _layernorm(x, g, b):
            mu = jnp.mean(x, axis=-1, keepdims=True)
            var = jnp.mean(jnp.square(x - mu), axis=-1, keepdims=True)
            return (x - mu) * jax.lax.rsqrt(var + LN_EPS) * g + b
        key = jax.random.key(seed)
        ks = jax.random.split(key, 16)
        inp = {'x': jax.random.normal(ks[0], (N, IN_DIM), dtype=jnp.float32), 'edge_index': jax.random.randint(ks[1], (2, E), 0, N, dtype=jnp.int32), 'W0': jax.random.normal(ks[2], (IN_DIM, HID), dtype=jnp.float32) * 0.05, 'b0': jnp.zeros((HID,), dtype=jnp.float32), 'W1': jax.random.normal(ks[3], (HID, HID), dtype=jnp.float32) * 0.05, 'b1': jnp.zeros((HID,), dtype=jnp.float32), 'W2': jax.random.normal(ks[4], (HID, HID), dtype=jnp.float32) * 0.05, 'b2': jnp.zeros((HID,), dtype=jnp.float32), 'W3': jax.random.normal(ks[5], (HID, OUT_DIM), dtype=jnp.float32) * 0.05, 'b3': jnp.zeros((OUT_DIM,), dtype=jnp.float32), 'a0': jnp.ones((1,), dtype=jnp.float32), 'a1': jnp.ones((1,), dtype=jnp.float32), 'a2': jnp.ones((1,), dtype=jnp.float32), 'g0': jnp.ones((HID,), dtype=jnp.float32), 'beta0': jnp.zeros((HID,), dtype=jnp.float32), 'g1': jnp.ones((HID,), dtype=jnp.float32), 'beta1': jnp.zeros((HID,), dtype=jnp.float32), 'g2': jnp.ones((HID,), dtype=jnp.float32), 'beta2': jnp.zeros((HID,), dtype=jnp.float32)}
        return inp
    _L0_gnn_all = _L0_gnn_setup()
    _L0_gnn_in = {k: v for k, v in _L0_gnn_all.items() if k in ('W0', 'b0', 'W1', 'b1', 'W2', 'b2', 'W3', 'b3', 'a0', 'a1', 'a2', 'g0', 'beta0', 'g1', 'beta1', 'g2', 'beta2')}
    del _L0_gnn_all

    def _L1_gnn_setup():
        import jax, jax.numpy as jnp
        import numpy as np
        N, E, D, H, L, FF = (3125, 31250, 128, 8, 2, 512)
        HD = D // H

        def _layernorm(x, g, b):
            mu = jnp.mean(x, axis=-1, keepdims=True)
            var = jnp.mean(jnp.square(x - mu), axis=-1, keepdims=True)
            return (x - mu) * jax.lax.rsqrt(var + 1e-05) * g + b

        def _forward(edge_index, x, Wq, bq, Wk, bk, Wv, bv, Wo, bo, Wpos, bpos, Wdeg, bdeg, ln1_g, ln1_b, ln2_g, ln2_b, W1, b1, W2, b2):
            n = x.shape[0]
            loops = jnp.arange(n, dtype=edge_index.dtype)
            src = jnp.concatenate([edge_index[0], loops])
            dst = jnp.concatenate([edge_index[1], loops])
            scale = np.float32(np.sqrt(HD))
            for l in range(L):
                xn = _layernorm(x, ln1_g[l], ln1_b[l])
                deg = jax.ops.segment_sum(jnp.ones_like(src, dtype=x.dtype), src, num_segments=n)
                deg = (deg - deg.mean()) / (jnp.std(deg, ddof=1) + 1e-06)
                pos = xn @ Wpos[l] + bpos[l] + deg[:, None] * Wdeg[l][0] + bdeg[l]
                xp = xn + pos
                q = (xp @ Wq[l] + bq[l]).reshape(n, H, HD)
                k = (xp @ Wk[l] + bk[l]).reshape(n, H, HD)
                v = (xp @ Wv[l] + bv[l]).reshape(n, H, HD)
                att = jnp.einsum('ehd,ehd->eh', q[dst], k[src]) / scale
                att = jnp.nan_to_num(jnp.clip(att, -50.0, 50.0), nan=0.0, posinf=50.0, neginf=-50.0)
                m = jax.ops.segment_max(att, dst, num_segments=n)
                ex = jnp.exp(att - m[dst])
                s = jax.ops.segment_sum(ex, dst, num_segments=n)
                alpha = ex / (s[dst] + 1e-16)
                msg = (v[src] * alpha[:, :, None]).reshape(-1, D)
                aggr = jax.ops.segment_sum(msg, dst, num_segments=n)
                x = x + (aggr @ Wo[l] + bo[l])
                h = jax.nn.gelu(_layernorm(x, ln2_g[l], ln2_b[l]) @ W1[l] + b1[l], approximate=False)
                x = x + (h @ W2[l] + b2[l])
            return x
        key = jax.random.key(seed)
        ks = jax.random.split(key, 16)
        inp = {'x': jax.random.normal(ks[0], (N, D), jnp.float32), 'edge_index': jax.random.randint(ks[1], (2, E), 0, N, jnp.int32)}

        def w(k, shape, fan_in):
            return jax.random.normal(k, shape, jnp.float32) / np.float32(np.sqrt(fan_in))
        inp['Wq'] = w(ks[2], (L, D, D), D)
        inp['Wk'] = w(ks[3], (L, D, D), D)
        inp['Wv'] = w(ks[4], (L, D, D), D)
        inp['Wo'] = w(ks[5], (L, D, D), D)
        inp['Wpos'] = w(ks[6], (L, D, D), D)
        inp['Wdeg'] = w(ks[7], (L, 1, D), 1)
        inp['W1'] = w(ks[8], (L, D, FF), D)
        inp['W2'] = w(ks[9], (L, FF, D), FF)
        for name, shape in [('bq', (L, D)), ('bk', (L, D)), ('bv', (L, D)), ('bo', (L, D)), ('bpos', (L, D)), ('bdeg', (L, D)), ('ln1_b', (L, D)), ('ln2_b', (L, D)), ('b1', (L, FF)), ('b2', (L, D))]:
            inp[name] = jnp.zeros(shape, jnp.float32)
        inp['ln1_g'] = jnp.ones((L, D), jnp.float32)
        inp['ln2_g'] = jnp.ones((L, D), jnp.float32)
        return inp
    _L1_gnn_all = _L1_gnn_setup()
    _L1_gnn_in = {k: v for k, v in _L1_gnn_all.items() if k in ('Wq', 'bq', 'Wk', 'bk', 'Wv', 'bv', 'Wo', 'bo', 'Wpos', 'bpos', 'Wdeg', 'bdeg', 'ln1_g', 'ln1_b', 'ln2_g', 'ln2_b', 'W1', 'b1', 'W2', 'b2')}
    del _L1_gnn_all
    return {'x': x, 'src': src, 'dst': dst, 'L0_gnn_W0': _L0_gnn_in['W0'], 'L0_gnn_b0': _L0_gnn_in['b0'], 'L0_gnn_W1': _L0_gnn_in['W1'], 'L0_gnn_b1': _L0_gnn_in['b1'], 'L0_gnn_W2': _L0_gnn_in['W2'], 'L0_gnn_b2': _L0_gnn_in['b2'], 'L0_gnn_W3': _L0_gnn_in['W3'], 'L0_gnn_b3': _L0_gnn_in['b3'], 'L0_gnn_a0': _L0_gnn_in['a0'], 'L0_gnn_a1': _L0_gnn_in['a1'], 'L0_gnn_a2': _L0_gnn_in['a2'], 'L0_gnn_g0': _L0_gnn_in['g0'], 'L0_gnn_beta0': _L0_gnn_in['beta0'], 'L0_gnn_g1': _L0_gnn_in['g1'], 'L0_gnn_beta1': _L0_gnn_in['beta1'], 'L0_gnn_g2': _L0_gnn_in['g2'], 'L0_gnn_beta2': _L0_gnn_in['beta2'], 'L1_gnn_Wq': _L1_gnn_in['Wq'], 'L1_gnn_bq': _L1_gnn_in['bq'], 'L1_gnn_Wk': _L1_gnn_in['Wk'], 'L1_gnn_bk': _L1_gnn_in['bk'], 'L1_gnn_Wv': _L1_gnn_in['Wv'], 'L1_gnn_bv': _L1_gnn_in['bv'], 'L1_gnn_Wo': _L1_gnn_in['Wo'], 'L1_gnn_bo': _L1_gnn_in['bo'], 'L1_gnn_Wpos': _L1_gnn_in['Wpos'], 'L1_gnn_bpos': _L1_gnn_in['bpos'], 'L1_gnn_Wdeg': _L1_gnn_in['Wdeg'], 'L1_gnn_bdeg': _L1_gnn_in['bdeg'], 'L1_gnn_ln1_g': _L1_gnn_in['ln1_g'], 'L1_gnn_ln1_b': _L1_gnn_in['ln1_b'], 'L1_gnn_ln2_g': _L1_gnn_in['ln2_g'], 'L1_gnn_ln2_b': _L1_gnn_in['ln2_b'], 'L1_gnn_W1': _L1_gnn_in['W1'], 'L1_gnn_b1': _L1_gnn_in['b1'], 'L1_gnn_W2': _L1_gnn_in['W2'], 'L1_gnn_b2': _L1_gnn_in['b2']}

def reference(x, src, dst, L0_gnn_W0, L0_gnn_b0, L0_gnn_W1, L0_gnn_b1, L0_gnn_W2, L0_gnn_b2, L0_gnn_W3, L0_gnn_b3, L0_gnn_a0, L0_gnn_a1, L0_gnn_a2, L0_gnn_g0, L0_gnn_beta0, L0_gnn_g1, L0_gnn_beta1, L0_gnn_g2, L0_gnn_beta2, L1_gnn_Wq, L1_gnn_bq, L1_gnn_Wk, L1_gnn_bk, L1_gnn_Wv, L1_gnn_bv, L1_gnn_Wo, L1_gnn_bo, L1_gnn_Wpos, L1_gnn_bpos, L1_gnn_Wdeg, L1_gnn_bdeg, L1_gnn_ln1_g, L1_gnn_ln1_b, L1_gnn_ln2_g, L1_gnn_ln2_b, L1_gnn_W1, L1_gnn_b1, L1_gnn_W2, L1_gnn_b2):
    import jax
    import jax.numpy as jnp

    def _L0_gnn_ref(x, edge_index, W0, b0, W1, b1, W2, b2, W3, b3, a0, a1, a2, g0, beta0, g1, beta1, g2, beta2):
        import jax, jax.numpy as jnp
        import numpy as np
        N, E = (6250, 100000)
        IN_DIM, HID, OUT_DIM = (128, 256, 128)
        LN_EPS = 1e-05

        def _gcn_norm(edge_index, n_nodes):
            loops = jnp.arange(n_nodes, dtype=edge_index.dtype)
            src = jnp.concatenate([edge_index[0], loops])
            dst = jnp.concatenate([edge_index[1], loops])
            deg = jax.ops.segment_sum(jnp.ones_like(dst, dtype=jnp.float32), dst, num_segments=n_nodes)
            dinv = jnp.where(deg > 0, jax.lax.rsqrt(deg), 0.0)
            norm = dinv[src] * dinv[dst]
            return (src, dst, norm)

        def _gcn_conv(x, W, b, src, dst, norm, n_nodes):
            h = x @ W
            msg = h[src] * norm[:, None]
            out = jax.ops.segment_sum(msg, dst, num_segments=n_nodes)
            return out + b

        def _layernorm(x, g, b):
            mu = jnp.mean(x, axis=-1, keepdims=True)
            var = jnp.mean(jnp.square(x - mu), axis=-1, keepdims=True)
            return (x - mu) * jax.lax.rsqrt(var + LN_EPS) * g + b
        n_nodes = x.shape[0]
        src, dst, norm = _gcn_norm(edge_index, n_nodes)
        layers = [(W0, b0, a0, g0, beta0), (W1, b1, a1, g1, beta1), (W2, b2, a2, g2, beta2)]
        h = x
        for W, b, a, g, beta in layers:
            c = _gcn_conv(h, W, b, src, dst, norm, n_nodes)
            c = c * jax.nn.sigmoid(a)
            c = _layernorm(c, g, beta)
            h = jax.nn.elu(c)
        return _gcn_conv(h, W3, b3, src, dst, norm, n_nodes)

    def _L1_gnn_ref(x, edge_index, Wq, bq, Wk, bk, Wv, bv, Wo, bo, Wpos, bpos, Wdeg, bdeg, ln1_g, ln1_b, ln2_g, ln2_b, W1, b1, W2, b2):
        import jax, jax.numpy as jnp
        import numpy as np
        N, E, D, H, L, FF = (3125, 31250, 128, 8, 2, 512)
        HD = D // H

        def _layernorm(x, g, b):
            mu = jnp.mean(x, axis=-1, keepdims=True)
            var = jnp.mean(jnp.square(x - mu), axis=-1, keepdims=True)
            return (x - mu) * jax.lax.rsqrt(var + 1e-05) * g + b

        def _forward(edge_index, x, Wq, bq, Wk, bk, Wv, bv, Wo, bo, Wpos, bpos, Wdeg, bdeg, ln1_g, ln1_b, ln2_g, ln2_b, W1, b1, W2, b2):
            n = x.shape[0]
            loops = jnp.arange(n, dtype=edge_index.dtype)
            src = jnp.concatenate([edge_index[0], loops])
            dst = jnp.concatenate([edge_index[1], loops])
            scale = np.float32(np.sqrt(HD))
            for l in range(L):
                xn = _layernorm(x, ln1_g[l], ln1_b[l])
                deg = jax.ops.segment_sum(jnp.ones_like(src, dtype=x.dtype), src, num_segments=n)
                deg = (deg - deg.mean()) / (jnp.std(deg, ddof=1) + 1e-06)
                pos = xn @ Wpos[l] + bpos[l] + deg[:, None] * Wdeg[l][0] + bdeg[l]
                xp = xn + pos
                q = (xp @ Wq[l] + bq[l]).reshape(n, H, HD)
                k = (xp @ Wk[l] + bk[l]).reshape(n, H, HD)
                v = (xp @ Wv[l] + bv[l]).reshape(n, H, HD)
                att = jnp.einsum('ehd,ehd->eh', q[dst], k[src]) / scale
                att = jnp.nan_to_num(jnp.clip(att, -50.0, 50.0), nan=0.0, posinf=50.0, neginf=-50.0)
                m = jax.ops.segment_max(att, dst, num_segments=n)
                ex = jnp.exp(att - m[dst])
                s = jax.ops.segment_sum(ex, dst, num_segments=n)
                alpha = ex / (s[dst] + 1e-16)
                msg = (v[src] * alpha[:, :, None]).reshape(-1, D)
                aggr = jax.ops.segment_sum(msg, dst, num_segments=n)
                x = x + (aggr @ Wo[l] + bo[l])
                h = jax.nn.gelu(_layernorm(x, ln2_g[l], ln2_b[l]) @ W1[l] + b1[l], approximate=False)
                x = x + (h @ W2[l] + b2[l])
            return x
        return _forward(edge_index, x, Wq, bq, Wk, bk, Wv, bv, Wo, bo, Wpos, bpos, Wdeg, bdeg, ln1_g, ln1_b, ln2_g, ln2_b, W1, b1, W2, b2)
    edge_index = jnp.stack([src, dst])
    x = _layernorm(x + _L0_gnn_ref(x, edge_index, L0_gnn_W0, L0_gnn_b0, L0_gnn_W1, L0_gnn_b1, L0_gnn_W2, L0_gnn_b2, L0_gnn_W3, L0_gnn_b3, L0_gnn_a0, L0_gnn_a1, L0_gnn_a2, L0_gnn_g0, L0_gnn_beta0, L0_gnn_g1, L0_gnn_beta1, L0_gnn_g2, L0_gnn_beta2), axis=-1)
    x = _layernorm(x + _L1_gnn_ref(x, edge_index, L1_gnn_Wq, L1_gnn_bq, L1_gnn_Wk, L1_gnn_bk, L1_gnn_Wv, L1_gnn_bv, L1_gnn_Wo, L1_gnn_bo, L1_gnn_Wpos, L1_gnn_bpos, L1_gnn_Wdeg, L1_gnn_bdeg, L1_gnn_ln1_g, L1_gnn_ln1_b, L1_gnn_ln2_g, L1_gnn_ln2_b, L1_gnn_W1, L1_gnn_b1, L1_gnn_W2, L1_gnn_b2), axis=-1)
    return x

_drawn_inputs = setup_inputs


def setup_inputs(seed=0):
    import zlib

    import numpy as np

    out = dict(_drawn_inputs(seed))
    spreads = {'L0_gnn_b0': (0.0, 0.1),
     'L0_gnn_b1': (0.0, 0.1),
     'L0_gnn_b2': (0.0, 0.1),
     'L0_gnn_b3': (0.0, 0.1),
     'L0_gnn_g0': (1.0, 0.2),
     'L0_gnn_beta0': (0.0, 0.1),
     'L0_gnn_g1': (1.0, 0.2),
     'L0_gnn_beta1': (0.0, 0.1),
     'L0_gnn_g2': (1.0, 0.2),
     'L0_gnn_beta2': (0.0, 0.1),
     'L1_gnn_bq': (0.0, 0.1),
     'L1_gnn_bk': (0.0, 0.1),
     'L1_gnn_bv': (0.0, 0.1),
     'L1_gnn_bo': (0.0, 0.1),
     'L1_gnn_bpos': (0.0, 0.1),
     'L1_gnn_bdeg': (0.0, 0.1),
     'L1_gnn_ln1_g': (1.0, 0.2),
     'L1_gnn_ln1_b': (0.0, 0.1),
     'L1_gnn_ln2_g': (1.0, 0.2),
     'L1_gnn_ln2_b': (0.0, 0.1),
     'L1_gnn_b1': (0.0, 0.1),
     'L1_gnn_b2': (0.0, 0.1)}
    factors = {}
    for name, (base, spread) in spreads.items():
        noise = np.random.default_rng([zlib.crc32(name.encode()), seed]).standard_normal(out[name].shape)
        drawn = base * np.exp(spread * noise) if base else spread * noise
        out[name] = jnp.asarray(drawn.astype(out[name].dtype))
    for name, factor in factors.items():
        out[name] = (out[name] * factor).astype(out[name].dtype)
    return out
```

```python
from contextlib import ExitStack

import concourse.bass as bass
from concourse import mybir

F32 = mybir.dt.float32
BF16 = mybir.dt.bfloat16
I32 = mybir.dt.int32
ALU = mybir.AluOpType
ACT = mybir.ActivationFunctionType
AX_X = mybir.AxisListType.X

P = 128
GC = 4
RG = 4
RING = RG * GC
D = 128
HID = 256
KV = 2 * D
H = 8
HD = D // H
MSG = D + H
FF = 512
FC = FF // P
EPS = 1e-5
CLIP = 50.0
RSQRT_MAGIC = float(0x5F3759DF)

CONVS, PASSES = 4, 6
WIDTH = [D, HID, HID, D, KV, KV]

HIDDEN = {"sum_ready", "sum_turned", "sum_columns", "mixed", "gated", "normed", "elu_neg", "elu_parts", "rows_ready"}
PROJECT = {"xn_ready", "xn_turned", "xn_columns", "pos_mixed", "xp_columns", "qkv_mixed", "qkv_copied", "self_logits",
           "self_exp", "self_ready"}
FFN = {"sum_ready", "sum_turned", "sum_columns", "attended", "z_ready", "z_turned", "z_columns", "ff_mixed", "ff_gelu", "ff_out"}
STEPS = [
    HIDDEN,
    HIDDEN,
    HIDDEN | {"elu_turned", "elu_columns", "last_mixed", "last_rows"},
    {"sum_ready"} | PROJECT,
    FFN | PROJECT,
    FFN | {"out_ready"},
]


def seen(step, p, tiles, t):
    return tiles * sum(step in STEPS[q] for q in range(p)) + t + 1


class Steps:

    def __init__(self):
        self.here = 0

    def next(self):
        self.here += 1
        return self.here


def build_gnn(nc, w, out):
    n_nodes, d_in = w["x"].shape
    n_edges = (w["src_main"].shape[1]) * P + w["src_tail"].shape[0]
    assert d_in == D
    TILES = -(-n_nodes // P)
    ROWS = TILES * P
    LAST_ROWS = n_nodes - (TILES - 1) * P
    MAIN = w["src_main"].shape[1]
    TAIL = w["src_tail"].shape[0]
    LAPS = -(-n_edges // (P * RING))
    GROUPS = LAPS * RG
    COLS = GROUPS * GC
    HB = COLS // RING
    MAX_SEQ = GROUPS * TILES

    tables = [nc.dram_tensor(f"rows_{p}", [ROWS, WIDTH[p]], F32).ap() for p in range(PASSES)]
    with ExitStack() as ctx:
        def sb(name, shape, dt=F32):
            return ctx.enter_context(nc.sbuf_tensor(name, shape, dt))

        def psum(name):
            return ctx.enter_context(nc.psum_tensor(name, [P, 512], F32))

        def sem(name):
            return ctx.enter_context(nc.semaphore(name))

        x_sb = sb("x_sb", [P, TILES, D])
        own = sb("own", [P, TILES, HID])
        layer_x = own[:, :, 0:D]
        q_rows = own[:, :, D:KV]
        in_rows, in_cols = w["dst_rows"].shape
        early = sb("early", [P, max(TILES * MSG, 3 * in_cols + 5 * COLS)])
        own_msg = early[:, 0:TILES * MSG].rearrange("p (t m) -> p t m", m=MSG)
        here = early[0:in_rows, 0:in_cols].bitcast(I32)
        after = early[0:in_rows, in_cols:2 * in_cols].bitcast(I32)
        falls = early[0:in_rows, 2 * in_cols:3 * in_cols]
        digits = early[:, 3 * in_cols:3 * in_cols + 5 * COLS].rearrange("p (k c) -> p k c", k=5)
        hist_i = digits[:, 4, :].bitcast(I32)
        lo_f = digits[:, 0:2, :]
        hi_f = digits[:, 2:4, :]
        dinv = sb("dinv", [P, TILES])
        deg_dev = sb("deg_dev", [P, TILES])
        deg_n = sb("deg_n", [P, TILES])
        deg_diag = sb("deg_diag", [P, P])
        valid = sb("valid", [P, TILES])
        node_id = sb("node_id", [P, TILES])
        neg_first = sb("neg_first", [P, TILES])
        ids = sb("ids", [P, COLS], I32)
        src_idx = sb("src_idx", [P, COLS], I32)
        dst_i = sb("dst_i", [P, COLS], I32)
        dst_f = sb("dst_f", [P, GC + COLS])
        idx_stage = sb("idx_stage", [P, RING], I32)
        ring = sb("ring", [P, RING, KV])
        lane = sb("lane", [P, P])
        lane_bf = sb("lane_bf", [P, P], BF16)
        part = sb("part", [P, 1])
        ident = sb("ident", [P, P])
        ones = sb("ones", [P, P])
        zeros_bf = sb("zeros_bf", [P, P], BF16)
        tri = sb("tri", [TILES, TILES + 1])
        lane_t = sb("lane_t", [TILES, TILES + 1])
        conv_w = [sb("w0", [P, 1, HID]), sb("w1", [P, 2, HID]), sb("w2", [P, 2, HID]), sb("w3", [P, 2, D])]
        conv_b = [sb(f"b{i}", [1, HID]) for i in range(3)]
        b3_all = sb("b3_all", [P, D])
        gain = sb("gain", [P, 3, HID])
        shift = sb("shift", [P, 3, HID])
        gate_in = sb("gate_in", [P, 3])
        gate_e = sb("gate_e", [P, 3])
        gate_1 = sb("gate_1", [P, 3])
        gate = sb("gate", [P, 3])
        w_pos = sb("w_pos", [P, 2, D])
        w_pos1 = sb("w_pos1", [P, 2, D])
        w_deg = sb("w_deg", [P, 2, D])
        w_qkv = sb("w_qkv", [P, 2, 3 * D])
        b_qkv = sb("b_qkv", [1, 2, 3 * D])
        w_o = sb("w_o", [P, 2, D])
        b_o = sb("b_o", [1, 2, D])
        w_ff1 = sb("w_ff1", [P, 2, FF])
        w_ff2 = sb("w_ff2", [P, 2, FC, D])
        b_ff2 = sb("b_ff2", [1, 2, D])
        cols = sb("cols", [P, 6, 2])
        b_pd = sb("b_pd", [P, 2])
        b_ff1 = sb("b_ff1", [P, 2, FC])
        falls_1 = sb("falls_1", [in_rows, 1])
        flag = sb("flag", [1, 4])
        count_col = sb("count_col", [TILES, 1])
        start_i = sb("start_i", [1, TILES + 1], I32)
        start_g = sb("start_g", [1, TILES + 1], I32)
        start_f = sb("start_f", [1, TILES + 1])
        unsorted_start = sb("unsorted_start", [1, TILES + 1])
        unsorted_diff = sb("unsorted_diff", [1, TILES + 1])
        range_f = sb("range_f", [1, TILES + 1, 4])
        ranges = sb("ranges", [1, TILES + 1, 4], I32)
        lap_ids = sb("lap_ids", [1, TILES + 1])
        sweeps_f = sb("sweeps_f", [1, 2])
        sweeps_i = sb("sweeps_i", [1, 2], I32)
        one_lo = sb("one_lo", [P, RING, P], BF16)
        one_hi = sb("one_hi", [P, RING, 64], BF16)
        hist = sb("hist", [P, TILES])
        hist_src = sb("hist_src", [P, TILES])
        mask = sb("mask", [P, GC, P])
        mask_t = sb("mask_t", [P, GC, P])
        qk = sb("qk", [P, GC, D])
        dots = sb("dots", [P, GC, H])
        clip_a = sb("clip_a", [P, GC, H])
        clip_b = sb("clip_b", [P, GC, H])
        logits = sb("logits", [P, GC, H])
        msg = sb("msg", [P, GC, MSG])
        sums = sb("sums", [P, HID])
        sums_t = sb("sums_t", [P, 2, P])
        mixed_sb = sb("mixed_sb", [P, HID])
        xhat = sb("xhat", [P, HID])
        scaled = sb("scaled", [P, HID])
        y = sb("y", [P, HID])
        neg_part = sb("neg_part", [P, HID])
        exp_part = sb("exp_part", [P, HID])
        elu1 = sb("elu1", [P, HID])
        hidden = sb("hidden", [P, HID])
        elu_t = sb("elu_t", [P, 2, P])
        z = sb("z", [P, D])
        z1 = sb("z1", [P, D])
        zn = sb("zn", [P, D])
        zn_t = sb("zn_t", [P, P])
        xn = sb("xn", [P, D])
        xn_t = sb("xn_t", [P, P])
        xp_t = sb("xp_t", [P, P])
        kv_new = sb("kv_new", [P, KV])
        own_qk = sb("own_qk", [P, D])
        own_dots = sb("own_dots", [P, H])
        own_a = sb("own_a", [P, H])
        own_b = sb("own_b", [P, H])
        own_logits = sb("own_logits", [P, H])
        rden = sb("rden", [P, H])
        ff_t = sb("ff_t", [P, FC, P])
        stats = sb("stats", [P, 6])
        moments = sb("moments", [P, 2])
        rs_v = sb("rs_v", [P, TILES])
        rs_h = sb("rs_h", [P, TILES], I32)
        rs_y = sb("rs_y", [P, TILES], I32)
        rs_t = sb("rs_t", [P, TILES])
        rs_u = sb("rs_u", [P, TILES])
        sq = sb("sq", [P, TILES])
        sq_1 = sb("sq_1", [P, 1])
        std_f = sb("std_f", [P, 4])

        acc_ps = psum("acc_ps")
        turn_ps = psum("turn_ps")
        mix_ps = psum("mix_ps")
        mix2_ps = psum("mix2_ps")
        maskt_ps = [psum("maskt_ps0"), psum("maskt_ps1")]
        q_ps = [psum("q_ps0"), psum("q_ps1")]
        hist_ps, small_ps = maskt_ps

        loaded = sem("loaded")
        weights_loaded = sem("weights_loaded")
        consts_ready = sem("consts_ready")
        prep = sem("prep")
        prep_pe = sem("prep_pe")
        gate_exp = sem("gate_exp")
        onehots_ready = sem("onehots_ready")
        onehots_used = sem("onehots_used")
        hist_zeroed = sem("hist_zeroed")
        idx_staged = sem("idx_staged")
        staging_seen, slots_seen = sem("staging_seen"), sem("slots_seen")
        landed = [sem(f"landed_{j}") for j in range(RING)]
        group_landed = sem("group_landed")
        groups_freed = sem("groups_freed")
        masks_ready = sem("masks_ready")
        masks_used = sem("masks_used")
        masks_turned = sem("masks_turned")
        mask_t_ready = sem("mask_t_ready")
        q_ready = sem("q_ready")
        edge_step = sem("edge_step")
        logits_ready = sem("logits_ready")
        exp_ready = sem("exp_ready")
        msg_ready = sem("msg_ready")
        tile_step = sem("tile_step")
        rows_written = sem("rows_written")
        out_written = sem("out_written")
        step = {s: sem(s) for s in sorted(set().union(*STEPS))}

        block = ctx.enter_context(nc.Block())

        def pass_base(p, sweeps):
            return p * GROUPS * sweeps

        def visit(p, sweeps, t, g):
            return p * (GROUPS * sweeps + TILES - 1) + g + t

        def tile_range(eng, t):
            first = eng.value_load(ranges[0:1, bass.ds(t, 1), 0:1].rearrange("a t c -> a (t c)"), min_val=0, max_val=MAX_SEQ)
            last = eng.value_load(ranges[0:1, bass.ds(t, 1), 1:2].rearrange("a t c -> a (t c)"), min_val=0, max_val=MAX_SEQ)
            return first, last

        LOADS_IN = 1 + 4 + 2 + 2 + 1
        N_WEIGHTS = 4 + 9 + 1 + 2 * (6 + 7) + 2
        def rsqrt(v, wait, signal, n, width, eps):
            a, h, g, tt, u = rs_v[:, 0:width], rs_h[:, 0:width], rs_y[:, 0:width], rs_t[:, 0:width], rs_u[:, 0:width]
            yf = g.bitcast(F32)
            vec = nc.vector
            vec.tensor_scalar(a, v, 1.0, eps, ALU.mult, ALU.add).then_inc(signal, 1)
            wait(n.next())
            vec.tensor_scalar(h, a.bitcast(I32), 1, None, ALU.arith_shift_right).then_inc(signal, 1)
            wait(n.next())
            vec.tensor_scalar(g, h, -1.0, RSQRT_MAGIC, ALU.mult, ALU.add).then_inc(signal, 1)
            wait(n.next())
            for _ in range(3):
                vec.tensor_tensor(tt, yf, yf, ALU.mult).then_inc(signal, 1) if width > 1 else \
                    vec.scalar_tensor_tensor(out=u, in0=a, scalar=yf, in1=yf, op0=ALU.mult, op1=ALU.mult).then_inc(signal, 1)
                wait(n.next())
                if width > 1:
                    vec.tensor_tensor(u, tt, a, ALU.mult).then_inc(signal, 1)
                    wait(n.next())
                vec.tensor_scalar(tt, u, -0.5, 1.5, ALU.mult, ALU.add).then_inc(signal, 1)
                wait(n.next())
                vec.tensor_tensor(yf, yf, tt, ALU.mult).then_inc(signal, 1)
                wait(n.next())
            return yf

        done = {}

        @block.vector
        def _(vec):
            def ready(count):
                vec.wait_ge(prep, count)
            n = Steps()
            vec.wait_ge(consts_ready, 2)
            vec.tensor_scalar(ident[:, :], lane[:, :], part[:, 0:1], None, ALU.is_equal).then_inc(prep, 1)
            n.next()
            vec.tensor_scalar(tri[:, :], lane_t[:, :], part[0:TILES, 0:1], None, ALU.is_gt).then_inc(prep, 1)
            n.next()
            vec.tensor_scalar(valid[:, :], node_id[:, :], float(n_nodes), None, ALU.is_lt).then_inc(prep, 1)
            n.next()
            vec.memset(unsorted_start[:, 0:1], 0.0).then_inc(prep, 1)
            n.next()
            vec.memset(dst_f[:, 0:GC], -1.0).then_inc(prep, 1)
            n.next()
            vec.memset(one_hi[:, :, :], 0.0).then_inc(prep, 1)
            n.next()
            vec.wait_ge(loaded, 16 * LOADS_IN)
            vec.tensor_copy(dst_f[:, GC:], dst_i[:, :]).then_inc(prep, 1)
            n.next()
            vec.tensor_scalar(src_idx[:, :], ids[:, :], 0.0, None, ALU.max).then_inc(prep, 1)
            n.next()
            for e, id_array in ((0, dst_i), (1, ids)):
                vec.tensor_scalar(hist_i[:, :], id_array[:, :], P - 1, None, ALU.bitwise_and).then_inc(prep, 1)
                ready(n.next())
                vec.tensor_copy(lo_f[:, e, :], hist_i[:, :]).then_inc(prep, 1)
                ready(n.next())
                vec.tensor_scalar(hist_i[:, :], id_array[:, :], P.bit_length() - 1, None, ALU.arith_shift_right).then_inc(prep, 1)
                ready(n.next())
                vec.tensor_copy(hi_f[:, e, :], hist_i[:, :]).then_inc(prep, 1)
                ready(n.next())

            def onehots(e, b):
                for h in range(2):
                    vec.wait_ge(onehots_used, (HB * e + b) * 2 + h + 1)
                    for j in range(h * RING // 2, (h + 1) * RING // 2):
                        vec.tensor_scalar(one_lo[:, j, :], lane_bf[:, :], lo_f[:, e, bass.ds(b * RING + j, 1)], None, ALU.is_equal)
                        last = vec.tensor_scalar(one_hi[:, j, 0:TILES], lane_bf[:, 0:TILES], hi_f[:, e, bass.ds(b * RING + j, 1)], None, ALU.is_equal)
                    last.then_inc(onehots_ready, 1)

            with vec.Fori(0, HB) as b:
                onehots(0, b)
            vec.wait_ge(prep_pe, 1)
            vec.tensor_copy(hist[:, :], hist_ps[:, 0:TILES]).then_inc(prep, 1)
            n.next()
            yf = rsqrt(hist_ps[:, 0:TILES], ready, prep, n, TILES, 1.0)
            vec.tensor_copy(dinv[:, :], yf).then_inc(prep, 1)
            ready(n.next())
            for t0 in range(0, TILES, 7):
                t1 = min(TILES, t0 + 7)
                vec.tensor_tensor(own[:, t0:t1, 0:D], x_sb[:, t0:t1, :],
                                  dinv[:, t0:t1].unsqueeze(2).broadcast_to([P, t1 - t0, D]), ALU.mult).then_inc(prep, 1)
                n.next()
            done["rows"] = n.here
            vec.tensor_tensor(falls[:, :], here[:, :], after[:, :], ALU.is_gt).then_inc(prep, 1)
            ready(n.next())
            vec.tensor_reduce(falls_1[:, :], falls[:, :], AX_X, ALU.add).then_inc(prep, 1)
            ready(n.next())
            done["falls"] = n.here
            vec.wait_ge(prep_pe, 2)
            vec.tensor_scalar(flag[:, 0:1], small_ps[0:1, 0:1], 0.0, None, ALU.is_gt).then_inc(prep, 1)
            ready(n.next())
            vec.tensor_copy(count_col[:, :], small_ps[0:TILES, 1:2]).then_inc(prep, 1)
            ready(n.next())
            done["counts"] = n.here
            vec.wait_ge(prep_pe, 3)
            vec.tensor_copy(start_i[:, :], small_ps[0:1, 64:64 + TILES + 1]).then_inc(prep, 1)
            ready(n.next())
            vec.tensor_scalar(start_g[:, :], start_i[:, :], (P * GC).bit_length() - 1, None, ALU.arith_shift_right).then_inc(prep, 1)
            ready(n.next())
            vec.tensor_copy(start_f[:, :], start_g[:, :]).then_inc(prep, 1)
            ready(n.next())
            vec.memset(start_f[:, TILES:TILES + 1], float(GROUPS - 1)).then_inc(prep, 1)
            ready(n.next())
            vec.tensor_tensor(unsorted_diff[:, :], unsorted_start[:, :], start_f[:, :], ALU.subtract).then_inc(prep, 1)
            ready(n.next())
            vec.scalar_tensor_tensor(out=range_f[:, :, 0], in0=unsorted_diff[:, :], scalar=flag[:, 0:1], in1=start_f[:, :],
                                     op0=ALU.mult, op1=ALU.add).then_inc(prep, 1)
            ready(n.next())
            vec.tensor_copy(range_f[:, 0:TILES, 1], range_f[:, 1:TILES + 1, 0]).then_inc(prep, 1)
            ready(n.next())
            vec.tensor_scalar(lap_ids[:, :], lap_ids[:, :], flag[:, 0:1], -1.0, ALU.mult, ALU.mult).then_inc(prep, 1)
            ready(n.next())
            vec.tensor_scalar(range_f[:, :, 2], lap_ids[:, :], 1.0, None, ALU.add).then_inc(prep, 1)
            ready(n.next())
            vec.tensor_scalar(sweeps_f[:, 0:1], flag[:, 0:1], float(TILES - 1), 1.0, ALU.mult, ALU.add).then_inc(prep, 1)
            ready(n.next())
            vec.tensor_copy(sweeps_i[:, 0:1], sweeps_f[:, 0:1]).then_inc(prep, 1)
            ready(n.next())
            vec.tensor_copy(ranges[:, :, :], range_f[:, :, :]).then_inc(prep, 1)
            ready(n.next())
            done["ranges"] = n.here
            with vec.Fori(0, HB) as b:
                onehots(1, b)
            vec.wait_ge(prep_pe, 4)
            vec.tensor_scalar(hist_src[:, :], hist_ps[:, 0:TILES], -float(n_edges) / n_nodes, None, ALU.add).then_inc(prep, 1)
            ready(n.next())
            vec.tensor_tensor(deg_dev[:, :], hist_src[:, :], valid[:, :], ALU.mult).then_inc(prep, 1)
            ready(n.next())
            vec.tensor_tensor(sq[:, :], deg_dev[:, :], deg_dev[:, :], ALU.mult).then_inc(prep, 1)
            ready(n.next())
            vec.tensor_reduce(sq_1[:, :], sq[:, :], AX_X, ALU.add).then_inc(prep, 1)
            ready(n.next())
            done["squares"] = n.here
            vec.wait_ge(prep_pe, 5)
            vec.tensor_scalar(std_f[:, 0:1], small_ps[:, 200:201], 1.0 / (n_nodes - 1), None, ALU.mult).then_inc(prep, 1)
            ready(n.next())
            r = rsqrt(std_f[:, 0:1], ready, prep, n, 1, 0.0)
            vec.tensor_scalar(std_f[:, 1:2], r, std_f[:, 0:1], 1e-6, ALU.mult, ALU.add).then_inc(prep, 1)
            ready(n.next())
            vec.reciprocal(std_f[:, 2:3], std_f[:, 1:2]).then_inc(prep, 1)
            ready(n.next())
            vec.tensor_scalar(deg_n[:, :], deg_dev[:, :], std_f[:, 2:3], None, ALU.mult).then_inc(prep, 1)
            ready(n.next())
            vec.wait_ge(weights_loaded, 16 * N_WEIGHTS)
            for l in range(2):
                vec.tensor_tensor(w_pos1[:, l, :], w_pos[:, l, :], ident[:, :], ALU.add).then_inc(prep, 1)
                ready(n.next())
            vec.tensor_tensor(b_pd[:, :], cols[:, 4, :], cols[:, 5, :], ALU.add).then_inc(prep, 1)
            ready(n.next())
            vec.wait_ge(gate_exp, 1)
            vec.tensor_scalar(gate_1[:, :], gate_e[:, :], 1.0, None, ALU.add).then_inc(prep, 1)
            ready(n.next())
            vec.reciprocal(gate[:, :], gate_1[:, :]).then_inc(prep, 1)
            ready(n.next())
            done["all"] = n.here

            sweeps = vec.value_load(sweeps_i[0:1, 0:1], min_val=1, max_val=TILES)

            def layernorm(to, v, m, signal):
                vec.bn_stats(stats[:, :], v).then_inc(tile_step, 1)
                vec.wait_ge(tile_step, m.next())
                vec.bn_aggr(moments[:, :], stats[:, :]).then_inc(tile_step, 1)
                vec.wait_ge(tile_step, m.next())
                r = rsqrt(moments[:, 1:2], lambda c: vec.wait_ge(tile_step, c), tile_step, m, 1, EPS)
                vec.tensor_scalar(to, v, moments[:, 0:1], r, ALU.subtract, ALU.mult).then_inc(signal, 1)

            def tile(p, t, first, last, shift_g):
                conv = p < CONVS
                F = WIDTH[p]

                def group(g, freed):
                    v = visit(p, sweeps, t, g)
                    col = nc.s_assert_within((g + shift_g) * GC, 0, COLS,
                                             skip_runtime_bounds_check_because="the ranges end with the sweep's last group")
                    for h in range(2):
                        vec.wait_ge(masks_used, v * 2 + h + 1)
                        for j in (2 * h, 2 * h + 1):
                            ins = vec.tensor_scalar(mask[:, j, :], lane[:, :], dst_f[:, bass.ds(col + j, 1)],
                                                    neg_first[:, bass.ds(t, 1)], ALU.subtract, ALU.is_equal)
                        ins.then_inc(masks_ready, 1)
                    if conv:
                        return
                    a = visit(p - CONVS, sweeps, t, g)
                    slot = (g & (RG - 1)) * GC
                    vec.wait_ge(group_landed, pass_base(p, sweeps) + g + 1)
                    for h in range(2):
                        vec.wait_ge(q_ready, a * 2 + h + 1)
                        vec.tensor_tensor(qk[:, 2 * h:2 * h + 2, :], q_ps[h][:, 0:2 * D].rearrange("p (c f) -> p c f", c=2),
                                          ring[:, bass.ds(slot + 2 * h, 2), 0:D], ALU.mult).then_inc(edge_step, 1)
                    for h in range(2):
                        vec.wait_ge(edge_step, h + 1)
                        vec.tensor_reduce(dots[:, 2 * h:2 * h + 2, :], qk[:, 2 * h:2 * h + 2, :].rearrange("p c (h d) -> p c h d", h=H),
                                          AX_X, ALU.add).then_inc(edge_step, 1)
                    vec.wait_ge(edge_step, 4)
                    vec.tensor_scalar(clip_a[:, :, :], dots[:, :, :], -4 * CLIP, 4 * CLIP, ALU.max, ALU.min).then_inc(edge_step, 1)
                    vec.tensor_scalar(clip_b[:, :, :], dots[:, :, :], 4 * CLIP, -4 * CLIP, ALU.min, ALU.max).then_inc(edge_step, 1)
                    vec.wait_ge(edge_step, 6)
                    vec.sem_clear(edge_step)
                    vec.tensor_tensor(logits[:, :, :], clip_a[:, :, :], clip_b[:, :, :], ALU.add).then_inc(logits_ready, 1)
                    vec.wait_ge(exp_ready, a + 1)
                    for h in range(2):
                        vec.tensor_tensor(
                            msg[:, 2 * h:2 * h + 2, 0:D].rearrange("p c (h d) -> p c h d", h=H),
                            ring[:, bass.ds(slot + 2 * h, 2), D:KV].rearrange("p c (h d) -> p c h d", h=H),
                            msg[:, 2 * h:2 * h + 2, D:MSG].unsqueeze(3).broadcast_to([P, 2, H, HD]), ALU.mult).then_inc(msg_ready, 1)
                    if freed:
                        vec.wait_ge(msg_ready, a * 2 + 2)
                        vec.sem_inc(groups_freed, 1)

                with vec.If(first < last):
                    with vec.Fori(first, last) as g:
                        group(g, True)
                with vec.Else():
                    pass
                group(last, False)
                m = Steps()
                vec.wait_ge(masks_used, visit(p, sweeps, t, last) * 2 + 4)
                if p < 3:
                    vec.tensor_scalar(sums[:, 0:F], acc_ps[:, 0:F], dinv[:, bass.ds(t, 1)], None, ALU.mult).then_inc(step["sum_ready"], 1)
                    vec.wait_ge(step["gated"], seen("gated", p, TILES, t))
                    layernorm(xhat[:, :], mixed_sb[:, :], m, tile_step)
                    vec.wait_ge(tile_step, m.next())
                    vec.tensor_tensor(scaled[:, :], xhat[:, :], gain[:, p, :], ALU.mult).then_inc(tile_step, 1)
                    vec.wait_ge(tile_step, m.next())
                    vec.tensor_tensor(y[:, :], scaled[:, :], shift[:, p, :], ALU.add).then_inc(step["normed"], 1)
                    vec.wait_ge(step["elu_parts"], seen("elu_parts", p, TILES, t))
                    vec.scalar_tensor_tensor(out=elu1[:, :], in0=y[:, :], scalar=0.0, in1=exp_part[:, :],
                                             op0=ALU.max, op1=ALU.add).then_inc(tile_step, 1)
                    vec.wait_ge(tile_step, m.next())
                    if p < 2:
                        vec.tensor_scalar(own[:, bass.ds(t, 1), :].rearrange("p a f -> p (a f)"), elu1[:, :], -1.0,
                                          dinv[:, bass.ds(t, 1)], ALU.add, ALU.mult).then_inc(step["rows_ready"], 1)
                    else:
                        vec.tensor_scalar(hidden[:, :], elu1[:, :], -1.0, None, ALU.add).then_inc(step["rows_ready"], 1)
                        vec.wait_ge(step["last_mixed"], seen("last_mixed", p, TILES, t))
                        vec.tensor_scalar(own[:, bass.ds(t, 1), 0:D].rearrange("p a f -> p (a f)"), mix2_ps[:, 0:D],
                                          dinv[:, bass.ds(t, 1)], None, ALU.mult).then_inc(step["last_rows"], 1)
                    return

                x_t = x_sb[:, bass.ds(t, 1), :].rearrange("p a f -> p (a f)")
                lx_t = layer_x[:, bass.ds(t, 1), :].rearrange("p a f -> p (a f)")

                def project():
                    q_t = q_rows[:, bass.ds(t, 1), :].rearrange("p a f -> p (a f)")
                    vec.wait_ge(step["qkv_copied"], seen("qkv_copied", p, TILES, t))
                    vec.tensor_tensor(own_qk[:, :], q_t, kv_new[:, 0:D], ALU.mult).then_inc(tile_step, 1)
                    vec.wait_ge(tile_step, m.next())
                    vec.tensor_reduce(own_dots[:, :], own_qk[:, :].rearrange("p (h d) -> p h d", h=H), AX_X, ALU.add).then_inc(tile_step, 1)
                    vec.wait_ge(tile_step, m.next())
                    vec.tensor_scalar(own_a[:, :], own_dots[:, :], -4 * CLIP, 4 * CLIP, ALU.max, ALU.min).then_inc(tile_step, 1)
                    m.next()
                    vec.tensor_scalar(own_b[:, :], own_dots[:, :], 4 * CLIP, -4 * CLIP, ALU.min, ALU.max).then_inc(tile_step, 1)
                    vec.wait_ge(tile_step, m.next())
                    vec.tensor_tensor(own_logits[:, :], own_a[:, :], own_b[:, :], ALU.add).then_inc(step["self_logits"], 1)
                    vec.wait_ge(step["self_exp"], seen("self_exp", p, TILES, t))
                    vec.tensor_tensor(own_msg[:, bass.ds(t, 1), 0:D].rearrange("p a (h d) -> p (a h) d", h=H),
                                      kv_new[:, D:KV].rearrange("p (h d) -> p h d", h=H),
                                      own_msg[:, bass.ds(t, 1), D:MSG].rearrange("p a h -> p (a h)").unsqueeze(2).broadcast_to([P, H, HD]),
                                      ALU.mult).then_inc(step["self_ready"], 1)

                if p == 3:
                    vec.scalar_tensor_tensor(out=z[:, :], in0=acc_ps[:, 0:D], scalar=dinv[:, bass.ds(t, 1)], in1=x_t,
                                             op0=ALU.mult, op1=ALU.add).then_inc(step["sum_ready"], 1)
                    vec.wait_ge(step["sum_ready"], seen("sum_ready", p, TILES, t))
                    vec.tensor_tensor(z1[:, :], z[:, :], b3_all[:, :], ALU.add).then_inc(tile_step, 1)
                    vec.wait_ge(tile_step, m.next())
                    layernorm(x_t, z1[:, :], m, tile_step)
                    vec.wait_ge(tile_step, m.next())
                    layernorm(xn[:, :], x_t, m, step["xn_ready"])
                    project()
                    return

                vec.reciprocal(rden[:, :], acc_ps[:, D:MSG]).then_inc(tile_step, 1)
                vec.wait_ge(tile_step, m.next())
                vec.tensor_tensor(sums[:, 0:D].rearrange("p (h d) -> p h d", h=H), acc_ps[:, 0:D].rearrange("p (h d) -> p h d", h=H),
                                  rden[:, :].unsqueeze(2).broadcast_to([P, H, HD]), ALU.mult).then_inc(step["sum_ready"], 1)
                vec.wait_ge(step["attended"], seen("attended", p, TILES, t))
                res = x_t if p == CONVS else lx_t
                vec.tensor_tensor(z[:, :], mix_ps[:, 0:D], res, ALU.add).then_inc(tile_step, 1)
                vec.wait_ge(tile_step, m.next())
                layernorm(zn[:, :], z[:, :], m, step["z_ready"])
                vec.wait_ge(step["ff_out"], seen("ff_out", p, TILES, t))
                if p == CONVS:
                    vec.tensor_tensor(lx_t, mix_ps[:, D:2 * D], z[:, :], ALU.add).then_inc(tile_step, 1)
                    vec.wait_ge(tile_step, m.next())
                    layernorm(xn[:, :], lx_t, m, step["xn_ready"])
                    project()
                else:
                    vec.tensor_tensor(z1[:, :], mix_ps[:, D:2 * D], z[:, :], ALU.add).then_inc(tile_step, 1)
                    vec.wait_ge(tile_step, m.next())
                    vec.tensor_tensor(xn[:, :], z1[:, :], x_t, ALU.add).then_inc(tile_step, 1)
                    vec.wait_ge(tile_step, m.next())
                    layernorm(lx_t, xn[:, :], m, step["out_ready"])

            for p in range(PASSES):
                with vec.Fori(0, TILES) as t:
                    first, last = tile_range(vec, t)
                    shift_g = vec.value_load(ranges[0:1, bass.ds(t, 1), 2:3].rearrange("a t c -> a (t c)"), min_val=-MAX_SEQ, max_val=1)
                    tile(p, t, first, last, shift_g)
                    vec.sem_clear(tile_step)

        @block.sync
        def _(sp):
            sp.dma_start(here[:, :], w["dst_rows"]).then_inc(loaded, 16)
            sp.wait_ge(consts_ready, 1)
            flat = w["dst_flat"]
            sp.dma_start(dst_i[:, 0:MAIN], w["dst_main"]).then_inc(loaded, 16)
            sp.dma_start(dst_i[0:TAIL, MAIN:MAIN + 1], w["dst_tail"]).then_inc(loaded, 16)
            sp.dma_start(ids[:, 0:MAIN], w["src_main"]).then_inc(loaded, 16)
            sp.dma_start(ids[0:TAIL, MAIN:MAIN + 1], w["src_tail"]).then_inc(loaded, 16)
            k = (in_rows - 1) * in_cols
            sp.dma_start(after[0:in_rows - 1, :], flat[1:1 + k].rearrange("(r c) -> r c", c=in_cols)).then_inc(loaded, 16)
            sp.dma_start(after[in_rows - 1:in_rows, 0:in_cols - 1], flat[1 + k:n_edges].rearrange("(r c) -> r c", r=1)).then_inc(loaded, 16)
            sp.dma_start(x_sb[:, 0:TILES - 1, :], w["x"][0:(TILES - 1) * P, :].rearrange("(t p) f -> p t f", p=P)).then_inc(loaded, 16)
            sp.dma_start(x_sb[0:LAST_ROWS, TILES - 1, :], w["x"][(TILES - 1) * P:n_nodes, :]).then_inc(loaded, 16)
            sp.dma_start(gate_in[:, :], w["gates"].rearrange("(a n) -> a n", a=1).broadcast_to([P, 3])).then_inc(loaded, 16)

            def load(to, src):
                sp.dma_start(to, src).then_inc(weights_loaded, 16)
            for l in range(4):
                load(conv_w[l][:, :, :], w[f"L0_gnn_W{l}"].rearrange("(k p) n -> p k n", p=P))
            row = "(a n) -> a n"
            for l in range(3):
                load(conv_b[l][:, :], w[f"L0_gnn_b{l}"].rearrange(row, a=1))
                load(gain[:, l, :], w[f"L0_gnn_g{l}"].rearrange(row, a=1).broadcast_to([P, HID]))
                load(shift[:, l, :], w[f"L0_gnn_beta{l}"].rearrange(row, a=1).broadcast_to([P, HID]))
            load(b3_all[:, :], w["L0_gnn_b3"].rearrange(row, a=1).broadcast_to([P, D]))
            for l in range(2):
                for i, m in enumerate(("Wq", "Wk", "Wv")):
                    load(w_qkv[:, l, i * D:(i + 1) * D], w[f"L1_gnn_{m}"][l, :, :])
                for i, m in enumerate(("bq", "bk", "bv")):
                    load(b_qkv[:, l, i * D:(i + 1) * D], w[f"L1_gnn_{m}"][l:l + 1, :])
                load(w_ff2[:, l, :, :], w["L1_gnn_W2"][l, :, :].rearrange("(c p) n -> p c n", p=P))
                load(w_o[:, l, :], w["L1_gnn_Wo"][l, :, :])
                load(w_ff1[:, l, :], w["L1_gnn_W1"][l, :, :])
                load(w_pos[:, l, :], w["L1_gnn_Wpos"][l, :, :])
                load(w_deg[:, l, :], w["L1_gnn_Wdeg"][l, :, :].broadcast_to([P, D]))
                load(b_o[:, l, :], w["L1_gnn_bo"][l:l + 1, :])
                load(b_ff2[:, l, :], w["L1_gnn_b2"][l:l + 1, :])
            load(cols[:, :, :], w["layer_cols"])
            load(b_ff1[:, :, :], w["ff1_cols"])
            sp.wait_ge(prep, done["ranges"])
            sweeps = sp.value_load(sweeps_i[0:1, 0:1], min_val=1, max_val=TILES)
            for p in range(PASSES):
                with sp.Fori(0, sweeps) as s:
                    with sp.Fori(0, LAPS) as lap:
                        count = (p * sweeps + s) * LAPS + lap + 1
                        for q in range(RG):
                            for j in range(q * GC, (q + 1) * GC):
                                sp.wait_ge(landed[j], count * 16)
                            sp.sem_inc(group_landed, 1)
            sp.wait_ge(out_written, 16 * TILES)
            sp.wait_ge(rows_written, 16 * (TILES * (PASSES - 1) + 1))

        @block.gpsimd
        def _(pool):
            pool.memset(dst_i[:, :], -1)
            pool.memset(ids[:, :], -1)
            pool.memset(after[:, :], 1 << 30)
            pool.memset(x_sb[:, TILES - 1, :], 0.0)
            pool.drain().then_inc(consts_ready, 1)
            exact = dict(allow_small_or_imprecise_dtypes=True)
            pool.iota(lane[:, :], [[1, P]], base=0, channel_multiplier=0, **exact)
            pool.iota(lane_bf[:, :], [[1, P]], base=0, channel_multiplier=0, **exact)
            pool.iota(part[:, :], [[0, 1]], base=0, channel_multiplier=1, **exact)
            pool.iota(node_id[:, :], [[P, TILES]], base=0, channel_multiplier=1, **exact)
            pool.iota(neg_first[:, :], [[-P, TILES]], base=0, channel_multiplier=0, **exact)
            pool.iota(lane_t[:, :], [[1, TILES + 1]], base=0, channel_multiplier=0, **exact)
            pool.iota(unsorted_start[:, :], [[GROUPS, TILES + 1]], base=-1, channel_multiplier=0, **exact)
            pool.iota(lap_ids[:, :], [[GROUPS, TILES + 1]], base=0, channel_multiplier=0, **exact)
            pool.memset(ones[:, :], 1.0)
            pool.memset(zeros_bf[:, :], 0.0)
            pool.memset(range_f[:, :, :], 0.0)
            pool.drain().then_inc(consts_ready, 1)

            pool.wait_ge(prep, done["ranges"])
            sweeps = pool.value_load(sweeps_i[0:1, 0:1], min_val=1, max_val=TILES)
            for p in range(PASSES):
                pool.wait_ge(rows_written, 16 * (TILES * p + 1))
                if p > 0:
                    pool.sem_inc(groups_freed, 1)
                with pool.Fori(0, sweeps) as s:
                    with pool.Fori(0, LAPS) as lap:
                        n = s * LAPS + lap
                        pool.wait_ge(landed[RING - 1], (p * (LAPS * sweeps) + n) * 16)
                        pool.tensor_copy(idx_stage[:, :], src_idx[:, bass.ds(lap * RING, RING)]).then_inc(idx_staged, 1)
                        for q in range(RG):
                            if q == 0:
                                pool.wait_ge(idx_staged, p * (LAPS * sweeps) + n + 1)
                                pool.sem_inc(staging_seen, 1)
                            pool.wait_ge(groups_freed, p * (GROUPS * sweeps) + n * RG + q)
                            pool.sem_inc(slots_seen, 1)
                            for j in range(q * GC, (q + 1) * GC):
                                pool.indirect_dma_start(
                                    ring[:, j, 0:WIDTH[p]], None, tables[p][:, :],
                                    bass.IndirectOffsetOnAxis(ap=idx_stage[:, j:j + 1], axis=0),
                                ).then_inc(landed[j], 16)

        @block.scalar
        def _(act):
            act.wait_ge(loaded, 16 * LOADS_IN)
            act.activation(gate_e[:, :], gate_in[:, :], ACT.Exp, scale=-1.0).then_inc(gate_exp, 1)
            act.wait_ge(prep, done["rows"])
            act.dma_start(tables[0].rearrange("(t p) f -> p t f", p=P), own[:, :, 0:D]).then_inc(rows_written, 16)
            act.wait_ge(prep, done["all"])
            sweeps = act.value_load(sweeps_i[0:1, 0:1], min_val=1, max_val=TILES)

            def tile(p, t, first, last, is_last=False):
                def group(g, freed):
                    v = visit(p, sweeps, t, g)
                    if p < CONVS:
                        if freed:
                            act.wait_ge(masks_used, v * 2 + 4)
                            act.sem_inc(groups_freed, 1)
                        return
                    a = visit(p - CONVS, sweeps, t, g)
                    for h in range(2):
                        act.wait_ge(masks_turned, a * 2 + h + 1)
                        act.activation(mask_t[:, 2 * h:2 * h + 2, :], maskt_ps[h][:, 0:2 * P].rearrange("p (c n) -> p c n", c=2),
                                       ACT.Copy).then_inc(mask_t_ready, 1)
                    act.wait_ge(logits_ready, a + 1)
                    act.activation(msg[:, :, D:MSG], logits[:, :, :], ACT.Exp, scale=0.5 / HD ** 0.5).then_inc(exp_ready, 1)

                with act.If(first < last):
                    with act.Fori(first, last) as g:
                        group(g, True)
                with act.Else():
                    pass
                group(last, False)

                def project(l):
                    act.activation(deg_diag[:, :], ident[:, :], ACT.Copy, scale=deg_n[:, bass.ds(t, 1)])
                    act.wait_ge(step["xn_turned"], seen("xn_turned", p, TILES, t))
                    act.activation(xn_t[:, :], turn_ps[:, 0:P], ACT.Identity, scale=cols[:, 0, l:l + 1], bias=cols[:, 1, l:l + 1]).then_inc(step["xn_columns"], 1)
                    act.wait_ge(step["pos_mixed"], seen("pos_mixed", p, TILES, t))
                    act.activation(xp_t[:, :], mix_ps[:, 2 * D:3 * D], ACT.Identity, bias=b_pd[:, l:l + 1]).then_inc(step["xp_columns"], 1)
                    act.wait_ge(step["qkv_mixed"], seen("qkv_mixed", p, TILES, t))
                    act.activation(q_rows[:, bass.ds(t, 1), :].rearrange("p a f -> p (a f)"), mix2_ps[:, 0:D], ACT.Copy)
                    act.wait_ge(rows_written, 16 * (TILES * p + 1 + t))
                    act.activation(kv_new[:, :], mix2_ps[:, D:3 * D], ACT.Copy).then_inc(step["qkv_copied"], 1)
                    act.wait_ge(step["qkv_copied"], seen("qkv_copied", p, TILES, t))
                    act.dma_start(tables[p + 1][bass.ds(t * P, P), :], kv_new[:, :]).then_inc(rows_written, 16)
                    act.wait_ge(step["self_logits"], seen("self_logits", p, TILES, t))
                    act.activation(own_msg[:, bass.ds(t, 1), D:MSG].rearrange("p a h -> p (a h)"), own_logits[:, :], ACT.Exp,
                                   scale=0.5 / HD ** 0.5).then_inc(step["self_exp"], 1)

                if p < 3:
                    F = WIDTH[p]
                    act.wait_ge(step["sum_turned"], seen("sum_turned", p, TILES, t))
                    act.activation(sums_t[:, 0:F // P, :], turn_ps[:, 0:F].rearrange("p (k n) -> p k n", n=P), ACT.Copy).then_inc(step["sum_columns"], 1)
                    act.wait_ge(step["mixed"], seen("mixed", p, TILES, t))
                    act.activation(mixed_sb[:, :], mix_ps[:, 0:HID], ACT.Identity, scale=gate[:, p:p + 1]).then_inc(step["gated"], 1)
                    act.wait_ge(step["normed"], seen("normed", p, TILES, t))
                    act.activation(neg_part[:, :], y[:, :], ACT.Relu, scale=-1.0).then_inc(step["elu_neg"], 1)
                    act.wait_ge(step["elu_neg"], seen("elu_neg", p, TILES, t))
                    act.activation(exp_part[:, :], neg_part[:, :], ACT.Exp, scale=-1.0).then_inc(step["elu_parts"], 1)
                    if p == 2:
                        act.wait_ge(step["elu_turned"], seen("elu_turned", p, TILES, t))
                        act.activation(elu_t[:, :, :], turn_ps[:, 0:HID].rearrange("p (k n) -> p k n", n=P), ACT.Copy).then_inc(step["elu_columns"], 1)
                    rows = "last_rows" if p == 2 else "rows_ready"
                    act.wait_ge(step[rows], seen(rows, p, TILES, t))
                    act.dma_start(tables[p + 1][bass.ds(t * P, P), :],
                                  own[:, bass.ds(t, 1), 0:WIDTH[p + 1]].rearrange("p a f -> p (a f)")).then_inc(rows_written, 16)
                    return
                if p == 3:
                    project(0)
                    return
                l = p - CONVS
                act.wait_ge(step["sum_turned"], seen("sum_turned", p, TILES, t))
                act.activation(sums_t[:, 0, :], turn_ps[:, 0:P], ACT.Copy).then_inc(step["sum_columns"], 1)
                act.wait_ge(step["z_turned"], seen("z_turned", p, TILES, t))
                act.activation(zn_t[:, :], turn_ps[:, 0:P], ACT.Identity, scale=cols[:, 2, l:l + 1], bias=cols[:, 3, l:l + 1]).then_inc(step["z_columns"], 1)
                act.wait_ge(step["ff_mixed"], seen("ff_mixed", p, TILES, t))
                for c in range(FC):
                    ins = act.activation(ff_t[:, c, :], mix2_ps[:, c * P:(c + 1) * P], ACT.Gelu, bias=b_ff1[:, l, c:c + 1])
                ins.then_inc(step["ff_gelu"], 1)
                if l == 0:
                    project(1)
                    return
                act.wait_ge(step["out_ready"], seen("out_ready", p, TILES, t))
                n_out = LAST_ROWS if is_last else P
                act.dma_start(out[bass.ds(t * P, n_out), :] if not is_last else out[t * P:n_nodes, :],
                              layer_x[0:n_out, bass.ds(t, 1), :].rearrange("p a f -> p (a f)")).then_inc(out_written, 16)

            for p in range(PASSES):
                whole = TILES - (p == PASSES - 1)
                with act.Fori(0, whole) as t:
                    first, last = tile_range(act, t)
                    tile(p, t, first, last)
            first, last = tile_range(act, TILES - 1)
            tile(PASSES - 1, TILES - 1, first, last, is_last=True)

        @block.tensor
        def _(pe):
            pe.sem_inc(onehots_used, 2)
            pe.sem_inc(masks_used, 2)
            pe.sem_inc(groups_freed, RG - 1)
            pe.wait_ge(consts_ready, 2)

            def count(e):
                pe.matmul(hist_ps[:, 0:TILES], zeros_bf[:, :], zeros_bf[:, 0:TILES], start=True, stop=False)
                with pe.Fori(0, HB) as b:
                    for h in range(2):
                        pe.wait_ge(onehots_ready, (HB * e + b) * 2 + h + 1)
                        for j in range(h * RING // 2, (h + 1) * RING // 2):
                            ins = pe.matmul(hist_ps[:, 0:TILES], one_lo[:, j, :], one_hi[:, j, 0:TILES], start=False, stop=False)
                        ins.then_inc(onehots_used, 1)
                pe.matmul(hist_ps[:, 0:TILES], zeros_bf[:, :], zeros_bf[:, 0:TILES], start=False, stop=True).then_inc(prep_pe, 1)

            count(0)
            pe.wait_ge(prep, done["falls"])
            pe.matmul(small_ps[0:1, 0:1], falls_1[:, :], ones[0:in_rows, 0:1], start=True, stop=True)
            pe.matmul(small_ps[0:TILES, 1:2], hist[:, :], ones[:, 0:1], start=True, stop=True).then_inc(prep_pe, 1)
            pe.wait_ge(prep, done["counts"])
            pe.matmul(small_ps[0:1, 64:64 + TILES + 1], count_col[:, :], tri[:, :], start=True, stop=True).then_inc(prep_pe, 1)
            count(1)
            pe.wait_ge(prep, done["squares"])
            pe.matmul(small_ps[:, 200:201], ones[:, :], sq_1[:, :], start=True, stop=True).then_inc(prep_pe, 1)
            pe.wait_ge(prep, done["all"])
            sweeps = pe.value_load(sweeps_i[0:1, 0:1], min_val=1, max_val=TILES)

            def turn(to, v, signal=None):
                ins = pe.matmul(to, v, ident[:, :], start=True, stop=True)
                if signal is not None:
                    ins.then_inc(signal, 1)

            def tile(p, t, first, last):
                conv = p < CONVS
                F = WIDTH[p] if conv else MSG
                pe.wait_ge(step["sum_ready"], seen("sum_ready", p, TILES, t) - 1)
                mine = own[:, bass.ds(t, 1), 0:F] if conv else own_msg[:, bass.ds(t, 1), :]
                pe.matmul(acc_ps[:, 0:F], ident[:, :], mine.rearrange("p a f -> p (a f)"), start=True, stop=False)

                def group(g, final):
                    v = visit(p, sweeps, t, g)
                    slot = (g & (RG - 1)) * GC
                    if conv:
                        pe.wait_ge(group_landed, pass_base(p, sweeps) + g + 1)
                    else:
                        a = visit(p - CONVS, sweeps, t, g)
                        for h in range(2):
                            pe.wait_ge(masks_ready, v * 2 + h + 1)
                            for j in (2 * h, 2 * h + 1):
                                ins = pe.matmul(maskt_ps[h][:, (j % 2) * P:(j % 2 + 1) * P], mask[:, j, :], ident[:, :], start=True, stop=True)
                            ins.then_inc(masks_turned, 1)
                        q_t = q_rows[:, bass.ds(t, 1), :].rearrange("p a f -> p (a f)")
                        for h in range(2):
                            pe.wait_ge(mask_t_ready, a * 2 + h + 1)
                            for j in (2 * h, 2 * h + 1):
                                ins = pe.matmul(q_ps[h][:, (j % 2) * D:(j % 2 + 1) * D], mask_t[:, j, :], q_t, start=True, stop=True)
                            ins.then_inc(q_ready, 1)
                    for h in range(2):
                        if conv:
                            pe.wait_ge(masks_ready, v * 2 + h + 1)
                        else:
                            pe.wait_ge(msg_ready, a * 2 + h + 1)
                        for j in (2 * h, 2 * h + 1):
                            rhs = ring[:, bass.ds(slot + j, 1), 0:F].rearrange("p a f -> p (a f)") if conv else msg[:, j, :]
                            ins = pe.matmul(acc_ps[:, 0:F], mask[:, j, :], rhs, start=False, stop=final and j == GC - 1)
                        ins.then_inc(masks_used, 1)

                with pe.If(first < last):
                    with pe.Fori(first, last) as g:
                        group(g, False)
                with pe.Else():
                    pass
                group(last, True)

                def project(l):
                    pe.wait_ge(step["xn_ready"], seen("xn_ready", p, TILES, t))
                    turn(turn_ps[:, 0:P], xn[:, :], step["xn_turned"])
                    pe.wait_ge(step["xn_columns"], seen("xn_columns", p, TILES, t))
                    pos = mix_ps[:, 2 * D:3 * D]
                    pe.matmul(pos, w_pos1[:, l, :], xn_t[:, :], start=True, stop=False)
                    pe.matmul(pos, w_deg[:, l, :], deg_diag[:, :], start=False, stop=True).then_inc(step["pos_mixed"], 1)
                    pe.wait_ge(step["xp_columns"], seen("xp_columns", p, TILES, t))
                    pe.matmul(mix2_ps[:, 0:3 * D], xp_t[:, :], w_qkv[:, l, :], start=True, stop=False)
                    pe.matmul(mix2_ps[:, 0:3 * D], ones[0:1, :], b_qkv[:, l, :], start=False, stop=True).then_inc(step["qkv_mixed"], 1)

                if p == 3:
                    project(0)
                    return
                pe.wait_ge(step["sum_ready"], seen("sum_ready", p, TILES, t))
                K = F // P
                for k in range(K):
                    turn(turn_ps[:, k * P:(k + 1) * P], sums[:, k * P:(k + 1) * P], step["sum_turned"] if k == K - 1 else None)
                pe.wait_ge(step["sum_columns"], seen("sum_columns", p, TILES, t))
                if conv:
                    for k in range(K):
                        pe.matmul(mix_ps[:, 0:HID], sums_t[:, k, :], conv_w[p][:, k, :], start=k == 0, stop=False)
                    pe.matmul(mix_ps[:, 0:HID], ones[0:1, :], conv_b[p][:, :], start=False, stop=True).then_inc(step["mixed"], 1)
                    if p == 2:
                        pe.wait_ge(step["rows_ready"], seen("rows_ready", p, TILES, t))
                        turn(turn_ps[:, 0:P], hidden[:, 0:P])
                        turn(turn_ps[:, P:2 * P], hidden[:, P:2 * P], step["elu_turned"])
                        pe.wait_ge(step["elu_columns"], seen("elu_columns", p, TILES, t))
                        pe.matmul(mix2_ps[:, 0:D], elu_t[:, 0, :], conv_w[3][:, 0, :], start=True, stop=False)
                        pe.matmul(mix2_ps[:, 0:D], elu_t[:, 1, :], conv_w[3][:, 1, :], start=False, stop=True).then_inc(step["last_mixed"], 1)
                    return
                l = p - CONVS
                pe.matmul(mix_ps[:, 0:D], sums_t[:, 0, :], w_o[:, l, :], start=True, stop=False)
                pe.matmul(mix_ps[:, 0:D], ones[0:1, :], b_o[:, l, :], start=False, stop=True).then_inc(step["attended"], 1)
                pe.wait_ge(step["z_ready"], seen("z_ready", p, TILES, t))
                turn(turn_ps[:, 0:P], zn[:, :], step["z_turned"])
                pe.wait_ge(step["z_columns"], seen("z_columns", p, TILES, t))
                for c in range(FC):
                    ins = pe.matmul(mix2_ps[:, c * P:(c + 1) * P], w_ff1[:, l, c * P:(c + 1) * P], zn_t[:, :], start=True, stop=True)
                ins.then_inc(step["ff_mixed"], 1)
                pe.wait_ge(step["ff_gelu"], seen("ff_gelu", p, TILES, t))
                for c in range(FC):
                    pe.matmul(mix_ps[:, D:2 * D], ff_t[:, c, :], w_ff2[:, l, c, :], start=c == 0, stop=False)
                pe.matmul(mix_ps[:, D:2 * D], ones[0:1, :], b_ff2[:, l, :], start=False, stop=True).then_inc(step["ff_out"], 1)
                if l == 0:
                    project(1)

            for p in range(PASSES):
                pe.wait_ge(rows_written, 16 * (TILES * p + 1))
                if p >= CONVS:
                    pe.wait_ge(step["self_ready"], seen("self_ready", p - 1, TILES, TILES - 1))
                with pe.Fori(0, TILES) as t:
                    first, last = tile_range(pe, t)
                    tile(p, t, first, last)


def kernel(**inputs):
    import numpy as np
    import concourse.bacc as bacc
    from concourse.bass_utils import run_bass_kernel_spmd

    a = {k: np.ascontiguousarray(v) for k, v in inputs.items()}
    n_nodes, n_edges = a["x"].shape[0], a["src"].shape[0]
    main = n_edges // P
    w = {k: v for k, v in a.items() if k not in ("src", "dst") and not k.startswith("L0_gnn_a")}
    for k in ("L0_gnn_b0",):
        assert w[k].shape == (HID,)
    for k in ("src", "dst"):
        w[k + "_main"] = np.ascontiguousarray(a[k][:main * P].reshape(main, P).T)
        w[k + "_tail"] = np.ascontiguousarray(a[k][main * P:].reshape(-1, 1))
    rows = max(r for r in range(1, P + 1) if n_edges % r == 0)
    w["dst_rows"] = a["dst"].reshape(rows, n_edges // rows)
    w["dst_flat"] = a["dst"]
    w["gates"] = np.concatenate([a[f"L0_gnn_a{i}"] for i in range(3)])
    w["layer_cols"] = np.ascontiguousarray(np.stack([a[f"L1_gnn_{k}"] for k in ("ln1_g", "ln1_b", "ln2_g", "ln2_b", "bpos", "bdeg")]).transpose(2, 0, 1))
    w["ff1_cols"] = np.ascontiguousarray(a["L1_gnn_b1"].reshape(2, FC, P).transpose(2, 0, 1))

    nc = bacc.Bacc("TRN2", target_bir_lowering=False, num_devices=1)
    arrays, args = {}, {}
    for k, v in w.items():
        arrays["in_" + k] = v
        args[k] = nc.dram_tensor("in_" + k, v.shape, mybir.dt.from_np(v.dtype), kind="ExternalInput").ap()
    out = nc.dram_tensor("out_0", (n_nodes, D), F32, kind="ExternalOutput").ap()
    build_gnn(nc, args, out)
    r = run_bass_kernel_spmd(nc, [arrays], core_ids=[0])
    return r.results[0]["out_0"]
```

```python
from contextlib import ExitStack

import concourse.bass as bass
from concourse import mybir

F32 = mybir.dt.float32
BF16 = mybir.dt.bfloat16
I32 = mybir.dt.int32
ALU = mybir.AluOpType
ACT = mybir.ActivationFunctionType
AX_X = mybir.AxisListType.X

P = 128
GC = 4
RG = 7
RING = RG * GC
D = 128
HID = 256
KV = 2 * D
H = 8
HD = D // H
MSG = D + H
FF = 512
FC = FF // P
EPS = 1e-5
CLIP = 50.0
RSQRT_MAGIC = float(0x5F3759DF)

CONVS, PASSES = 4, 6
WIDTH = [D, HID, HID, D, KV, KV]



class Steps:

    def __init__(self):
        self.here = 0

    def next(self):
        self.here += 1
        return self.here


def build_gnn(nc, w, out):
    n_nodes, d_in = w["x"].shape
    n_edges = (w["src_main"].shape[1]) * P + w["src_tail"].shape[0]
    assert d_in == D
    TILES = -(-n_nodes // P)
    ROWS = TILES * P
    LAST_ROWS = n_nodes - (TILES - 1) * P
    MAIN = w["src_main"].shape[1]
    TAIL = w["src_tail"].shape[0]
    LAPS = 2 * -(-n_edges // (2 * P * RING))
    GROUPS = LAPS * RG
    COLS = GROUPS * GC
    HC = -(-COLS // TILES)
    DIGITS = HC * TILES
    TB = max(n for n in range(1, 8) if TILES % n == 0)
    NB = TILES // TB
    pairs = [(i, min(i + 2, TB)) for i in range(0, TB, 2)]
    fours = [(i, min(i + 4, TB)) for i in range(0, TB, 4)]
    halves = [r for r in ((0, (TB + 1) // 2), ((TB + 1) // 2, TB)) if r[0] < r[1]]
    U2, U4, UH = len(pairs), len(fours), len(halves)

    PER = {
        "acc_read": [TB] * PASSES,
        "turned": [U2, U2, 2 * U2, U4, 3 * U4, 2 * U4],
        "columns": [U2, U2, 2 * U2, U4, 3 * U4, 2 * U4],
        "mixed": [U2, U2, U2, 0, 0, 0],
        "gated": [U2, U2, U2, 0, 0, 0],
        "normed": [UH, UH, UH, 0, 0, 0],
        "elu_neg": [UH, UH, UH, 0, 0, 0],
        "elu_parts": [UH, UH, UH, 0, 0, 0],
        "hidden_ready": [0, 0, 1, 0, 0, 0],
        "last_mixed": [0, 0, U4, 0, 0, 0],
        "attended": [0, 0, 0, 0, U4, U4],
        "z_ready": [0, 0, 0, 0, 1, 1],
        "ff_mixed": [0, 0, 0, 0, U4 * FC, U4 * FC],
        "ff_gelu": [0, 0, 0, 0, U4 * FC, U4 * FC],
        "ff_out": [0, 0, 0, 0, U4, U4],
        "xn_ready": [0, 0, 0, 1, 1, 0],
        "pos_mixed": [0, 0, 0, U4, U4, 0],
        "xp_columns": [0, 0, 0, U4, U4, 0],
        "qkv_mixed": [0, 0, 0, TB, TB, 0],
        "qkv_copied": [0, 0, 0, TB, TB, 0],
        "self_logits": [0, 0, 0, 1, 1, 0],
        "self_exp": [0, 0, 0, 1, 1, 0],
        "nodes_done": [1] * PASSES,
    }

    def at(step_name, p, b, k):
        return NB * sum(PER[step_name][:p]) + b * PER[step_name][p] + k

    MAX_SEQ = GROUPS * TILES

    tables = [nc.dram_tensor(f"rows_{p}", [ROWS, WIDTH[p]], F32).ap() for p in range(PASSES)]
    with ExitStack() as ctx:
        def sb(name, shape, dt=F32):
            return ctx.enter_context(nc.sbuf_tensor(name, shape, dt))

        def psum(name):
            return ctx.enter_context(nc.psum_tensor(name, [P, 512], F32))

        def sem(name):
            return ctx.enter_context(nc.semaphore(name))

        x_sb = sb("x_sb", [P, TILES, D])
        own = sb("own", [P, TILES, HID])
        layer_x = own[:, :, 0:D]
        q_rows = own[:, :, D:KV]
        LO, HI = HC * P // 2, (HC * TILES + 1) // 2
        early = sb("early", [P, max(TILES * MSG, 5 * DIGITS + LO + HI)])
        own_msg = early[:, 0:TILES * MSG].rearrange("p (t m) -> p t m", m=MSG)
        digits = early[:, 0:5 * DIGITS].rearrange("p (k c) -> p k c", k=5)
        hist_i = digits[:, 4, :].bitcast(I32)
        lo_f = digits[:, 0:2, :]
        hi_f = digits[:, 2:4, :]
        one_lo = early[:, 5 * DIGITS:5 * DIGITS + LO].bitcast(BF16).rearrange("p (j n) -> p j n", n=P)
        one_hi = early[:, 5 * DIGITS + LO:5 * DIGITS + LO + HI].bitcast(BF16)[:, 0:HC * TILES].rearrange("p (j n) -> p j n", n=TILES)
        dinv = sb("dinv", [P, TILES])
        deg_dev = sb("deg_dev", [P, TILES])
        deg_n = sb("deg_n", [P, TILES])
        valid = sb("valid", [P, TILES])
        node_id = sb("node_id", [P, TILES])
        neg_first = sb("neg_first", [P, TILES])
        src_idx = sb("src_idx", [P, COLS + RING], I32)
        dst_f = sb("dst_f", [P, GC + COLS])
        idx_stage = sb("idx_stage", [P, 2, RING], I32)
        ring = sb("ring", [P, RING, KV])
        lane = sb("lane", [P, P])
        lane_bf = sb("lane_bf", [P, P], BF16)
        part = sb("part", [P, 1])
        ident = sb("ident", [P, P])
        ident_bf = sb("ident_bf", [P, P], BF16)
        ones = sb("ones", [P, P])
        zeros_bf = sb("zeros_bf", [P, P], BF16)
        tri = sb("tri", [TILES, TILES + 1])
        lane_t = sb("lane_t", [TILES, TILES + 1])
        conv_w = [sb("w0", [P, 1, HID]), sb("w1", [P, 2, HID]), sb("w2", [P, 2, HID]), sb("w3", [P, 2, D])]
        bias_rows = sb("bias_rows", [2 * 32 + 1, max(2 * 3 * D, 3 * HID, 4 * D)])
        b_qkv = bias_rows[0:1, 0:6 * D].rearrange("a (l n) -> a l n", l=2)
        conv_b = [bias_rows[32:33, i * HID:(i + 1) * HID] for i in range(3)]
        b_o = bias_rows[64:65, 0:2 * D].rearrange("a (l n) -> a l n", l=2)
        b_ff2 = bias_rows[64:65, 2 * D:4 * D].rearrange("a (l n) -> a l n", l=2)
        b3_all = sb("b3_all", [P, D])
        gain = sb("gain", [P, 3, HID])
        shift = sb("shift", [P, 3, HID])
        gate_in = sb("gate_in", [P, 3])
        gate_e = sb("gate_e", [P, 3])
        gate_1 = sb("gate_1", [P, 3])
        gate = sb("gate", [P, 3])
        w_pos = sb("w_pos", [P, 2, D])
        w_pos1 = w_pos
        w_deg = sb("w_deg", [P, 2, D])
        w_qkv = sb("w_qkv", [P, 2, 3 * D])
        w_o = sb("w_o", [P, 2, D])
        w_ff1 = sb("w_ff1", [P, 2, FF])
        w_ff2 = sb("w_ff2", [P, 2, FC, D])
        cols = sb("cols", [P, 6, 2])
        b_pd = sb("b_pd", [P, 2])
        b_ff1 = sb("b_ff1", [P, 2, FC])
        falls_1 = sb("falls_1", [w["dst_rows"].shape[0], 1])
        flag = sb("flag", [1, 4])
        count_col = sb("count_col", [TILES, 1])
        start_i = sb("start_i", [1, TILES + 1], I32)
        start_g = sb("start_g", [1, TILES + 1], I32)
        start_f = sb("start_f", [1, TILES + 1])
        unsorted_start = sb("unsorted_start", [1, TILES + 1])
        unsorted_diff = sb("unsorted_diff", [1, TILES + 1])
        range_f = sb("range_f", [1, TILES + 1, 4])
        ranges = sb("ranges", [1, TILES + 1, 4], I32)
        lap_ids = sb("lap_ids", [1, TILES + 1])
        sweeps_f = sb("sweeps_f", [1, 2])
        sweeps_i = sb("sweeps_i", [1, 2], I32)
        hist = sb("hist", [P, TILES])
        hist_src = sb("hist_src", [P, TILES])
        mask = sb("mask", [P, GC, P])
        mask_bf = sb("mask_bf", [P, 2, GC, P], BF16)
        mask_t = sb("mask_t", [P, GC, P])
        dots = sb("dots", [P, GC, H])
        clip_a = sb("clip_a", [P, GC, H])
        clip_b = sb("clip_b", [P, GC, H])
        logits = sb("logits", [P, GC, H])
        msg = sb("msg", [P, GC, MSG])
        rows = sb("rows", [P, max(TB * HID, w["dst_rows"].shape[1])])
        rows_a = rows[:, 0:TB * HID].rearrange("p (t f) -> p t f", f=HID)
        falls_sb = rows
        turn_b = sb("turn_b", [P, TB, P])
        in_rows, in_cols = w["dst_rows"].shape
        wide = sb("wide", [P, max(TB * FF, TB * (KV + D) + GC * D, 2 * DIGITS + 2 * in_cols)])
        exp_part = wide[:, 0:TB * HID].rearrange("p (t f) -> p t f", f=HID)
        conv_t = wide[:, TB * HID:TB * FF].rearrange("p (t n) -> p t n", n=P)
        ff_t = wide[:, 0:TB * FF].rearrange("p (c n) -> p c n", c=FC)
        kv_new = exp_part
        deg_diag = wide[:, TB * KV:TB * (KV + D)].rearrange("p (t f) -> p t f", f=D)
        own_qk = wide[:, TB * (KV + D):TB * FF].rearrange("p (t f) -> p t f", f=D)
        qk = wide[:, TB * (KV + D):TB * (KV + D) + GC * D].rearrange("p (c f) -> p c f", f=D)
        xp_t = own_qk
        dst_i = wide[:, 0:DIGITS].bitcast(I32)
        ids = wide[:, DIGITS:2 * DIGITS].bitcast(I32)
        here = wide[0:in_rows, 2 * DIGITS:2 * DIGITS + in_cols].bitcast(I32)
        after = wide[0:in_rows, 2 * DIGITS + in_cols:2 * DIGITS + 2 * in_cols].bitcast(I32)
        falls = falls_sb[0:in_rows, 0:in_cols]
        warm = sb("warm", [P, 1])
        own_dots = sb("own_dots", [P, TB, H])
        own_a = sb("own_a", [P, TB, H])
        own_b = sb("own_b", [P, TB, H])
        own_logits = sb("own_logits", [P, TB, H])
        rden = sb("rden", [P, H])
        stats = sb("stats", [P, TB, 6])
        moments = sb("moments", [P, TB, 2])
        rs_v = sb("rs_v", [P, TILES])
        rs_h = sb("rs_h", [P, TILES], I32)
        rs_y = sb("rs_y", [P, TILES], I32)
        rs_t = sb("rs_t", [P, TILES])
        sq = sb("sq", [P, TILES])
        sq_1 = sb("sq_1", [P, 1])
        std_f = sb("std_f", [P, 4])

        acc_ps = psum("acc_ps")
        banks = [psum(f"bank_{i}") for i in range(7)]
        maskt_ps, q_ps = banks[0:2], banks[2:4]
        small_ps, hist_ps = banks[5:7]

        loaded = sem("loaded")
        weights_loaded = sem("weights_loaded")
        consts_ready = sem("consts_ready")
        prep = sem("prep")
        prep_pe = sem("prep_pe")
        gate_exp = sem("gate_exp")
        onehots_ready = sem("onehots_ready")
        onehots_used = sem("onehots_used")
        hist_zeroed = sem("hist_zeroed")
        idx_staged = sem("idx_staged")
        staging_seen, slots_seen = sem("staging_seen"), sem("slots_seen")
        batch_seen, banks_seen = sem("batch_seen"), sem("banks_seen")
        landed = [sem(f"landed_{j}") for j in range(RING)]
        group_landed = sem("group_landed")
        groups_freed = sem("groups_freed")
        masks_ready = sem("masks_ready")
        masks_used = sem("masks_used")
        mask_bf_ready = sem("mask_bf_ready")
        masks_turned = sem("masks_turned")
        mask_t_ready = sem("mask_t_ready")
        q_ready = sem("q_ready")
        q_used = sem("q_used")
        mask_kept, keep_seen = sem("mask_kept"), sem("keep_seen")
        edge_step = sem("edge_step")
        logits_ready = sem("logits_ready")
        exp_ready = sem("exp_ready")
        msg_ready = sem("msg_ready")
        msg_used = sem("msg_used")
        tile_step = sem("tile_step")
        rows_written = sem("rows_written")
        out_written = sem("out_written")
        step = {s: sem(s) for s in PER}

        block = ctx.enter_context(nc.Block())

        def pass_base(p, sweeps):
            return p * GROUPS * sweeps

        def visit(p, sweeps, t, g):
            return p * (GROUPS * sweeps + TILES - 1) + g + t

        def tile_range(eng, t):
            first = eng.value_load(ranges[0:1, bass.ds(t, 1), 0:1].rearrange("a t c -> a (t c)"), min_val=0, max_val=MAX_SEQ)
            last = eng.value_load(ranges[0:1, bass.ds(t, 1), 1:2].rearrange("a t c -> a (t c)"), min_val=0, max_val=MAX_SEQ)
            return first, last

        LOADS_IN = 1 + 4 + 2 + 2 + 1
        N_WEIGHTS = 4 + 9 + 1 + 2 * (6 + 7) + 2
        def rsqrt(v, wait, signal, n, width, eps):
            a, h, g, tt = rs_v[:, 0:width], rs_h[:, 0:width], rs_y[:, 0:width], rs_t[:, 0:width]
            yf = g.bitcast(F32)
            vec = nc.vector
            vec.tensor_scalar(a, v, 1.0, eps, ALU.mult, ALU.add).then_inc(signal, 1)
            wait(n.next())
            vec.tensor_scalar(h, a.bitcast(I32), 1, None, ALU.arith_shift_right).then_inc(signal, 1)
            wait(n.next())
            vec.tensor_scalar(g, h, -1.0, RSQRT_MAGIC, ALU.mult, ALU.add).then_inc(signal, 1)
            wait(n.next())
            vec.tensor_scalar(a, a, -0.5, None, ALU.mult).then_inc(signal, 1)
            wait(n.next())
            for _ in range(3):
                vec.tensor_tensor(tt, yf, yf, ALU.mult).then_inc(signal, 1)
                wait(n.next())
                vec.tensor_tensor(tt, tt, a, ALU.mult).then_inc(signal, 1)
                wait(n.next())
                vec.scalar_tensor_tensor(out=yf, in0=tt, scalar=1.5, in1=yf, op0=ALU.add, op1=ALU.mult).then_inc(signal, 1)
                wait(n.next())
            return yf

        done = {}

        @block.vector
        def _(vec):
            def ready(count):
                vec.wait_ge(prep, count)
            n = Steps()
            vec.wait_ge(consts_ready, 2)
            vec.tensor_scalar(ident[:, :], lane[:, :], part[:, 0:1], None, ALU.is_equal).then_inc(prep, 1)
            n.next()
            vec.tensor_scalar(ident_bf[:, :], lane[:, :], part[:, 0:1], None, ALU.is_equal).then_inc(prep, 1)
            n.next()
            vec.tensor_scalar(tri[:, :], lane_t[:, :], part[0:TILES, 0:1], None, ALU.is_gt).then_inc(prep, 1)
            n.next()
            vec.tensor_scalar(valid[:, :], node_id[:, :], float(n_nodes), None, ALU.is_lt).then_inc(prep, 1)
            n.next()
            vec.memset(unsorted_start[:, 0:1], 0.0).then_inc(prep, 1)
            n.next()
            vec.memset(dst_f[:, 0:GC], -1.0).then_inc(prep, 1)
            n.next()
            vec.wait_ge(loaded, 16 * LOADS_IN)
            vec.tensor_copy(dst_f[:, GC:], dst_i[:, 0:COLS]).then_inc(prep, 1)
            n.next()
            vec.tensor_scalar(src_idx[:, 0:COLS], ids[:, 0:COLS], 0.0, None, ALU.max).then_inc(prep, 1)
            n.next()
            vec.tensor_scalar(src_idx[:, COLS:], ids[:, 0:RING], 0.0, None, ALU.max).then_inc(prep, 1)
            n.next()
            for e, id_array in ((0, dst_i), (1, ids)):
                vec.tensor_scalar(hist_i[:, :], id_array[:, :], P - 1, None, ALU.bitwise_and).then_inc(prep, 1)
                ready(n.next())
                vec.tensor_copy(lo_f[:, e, :], hist_i[:, :]).then_inc(prep, 1)
                ready(n.next())
                vec.tensor_scalar(hist_i[:, :], id_array[:, :], P.bit_length() - 1, None, ALU.arith_shift_right).then_inc(prep, 1)
                ready(n.next())
                vec.tensor_copy(hi_f[:, e, :], hist_i[:, :]).then_inc(prep, 1)
                ready(n.next())

            hist_halves = [(0, HC // 2), (HC // 2, HC)]

            def onehots(e, b):
                for h, (j0, j1) in enumerate(hist_halves):
                    k = j1 - j0
                    vec.wait_ge(onehots_used, (TILES * e + b) * 2 + h + 1)
                    vec.tensor_tensor(one_lo[:, j0:j1, :], lane_bf[:, :].unsqueeze(1).broadcast_to([P, k, P]),
                                      lo_f[:, e, bass.ds(b * HC + j0, k)].unsqueeze(2).broadcast_to([P, k, P]), ALU.is_equal)
                    vec.tensor_tensor(one_hi[:, j0:j1, :], lane_bf[:, 0:TILES].unsqueeze(1).broadcast_to([P, k, TILES]),
                                      hi_f[:, e, bass.ds(b * HC + j0, k)].unsqueeze(2).broadcast_to([P, k, TILES]),
                                      ALU.is_equal).then_inc(onehots_ready, 1)

            with vec.Fori(0, TILES) as b:
                onehots(0, b)
            vec.wait_ge(prep_pe, 1)
            vec.tensor_copy(hist[:, :], hist_ps[:, 0:TILES]).then_inc(prep, 1)
            n.next()
            yf = rsqrt(hist_ps[:, 0:TILES], ready, prep, n, TILES, 1.0)
            vec.tensor_copy(dinv[:, :], yf).then_inc(prep, 1)
            ready(n.next())
            for t0 in range(0, TILES, 7):
                t1 = min(TILES, t0 + 7)
                vec.tensor_tensor(own[:, t0:t1, 0:D], x_sb[:, t0:t1, :],
                                  dinv[:, t0:t1].unsqueeze(2).broadcast_to([P, t1 - t0, D]), ALU.mult).then_inc(prep, 1)
                n.next()
            done["rows"] = n.here
            vec.tensor_tensor(falls[:, :], here[:, :], after[:, :], ALU.is_gt).then_inc(prep, 1)
            ready(n.next())
            vec.tensor_reduce(falls_1[:, :], falls[:, :], AX_X, ALU.add).then_inc(prep, 1)
            ready(n.next())
            done["falls"] = n.here
            vec.wait_ge(prep_pe, 2)
            vec.tensor_scalar(flag[:, 0:1], small_ps[0:1, 0:1], 0.0, None, ALU.is_gt).then_inc(prep, 1)
            ready(n.next())
            vec.tensor_copy(count_col[:, :], small_ps[0:TILES, 1:2]).then_inc(prep, 1)
            ready(n.next())
            done["counts"] = n.here
            vec.wait_ge(prep_pe, 3)
            vec.tensor_copy(start_i[:, :], small_ps[0:1, 64:64 + TILES + 1]).then_inc(prep, 1)
            ready(n.next())
            vec.tensor_scalar(start_g[:, :], start_i[:, :], (P * GC).bit_length() - 1, None, ALU.arith_shift_right).then_inc(prep, 1)
            ready(n.next())
            vec.tensor_copy(start_f[:, :], start_g[:, :]).then_inc(prep, 1)
            ready(n.next())
            vec.memset(start_f[:, TILES:TILES + 1], float(GROUPS - 1)).then_inc(prep, 1)
            ready(n.next())
            vec.tensor_tensor(unsorted_diff[:, :], unsorted_start[:, :], start_f[:, :], ALU.subtract).then_inc(prep, 1)
            ready(n.next())
            vec.scalar_tensor_tensor(out=range_f[:, :, 0], in0=unsorted_diff[:, :], scalar=flag[:, 0:1], in1=start_f[:, :],
                                     op0=ALU.mult, op1=ALU.add).then_inc(prep, 1)
            ready(n.next())
            vec.tensor_copy(range_f[:, 0:TILES, 1], range_f[:, 1:TILES + 1, 0]).then_inc(prep, 1)
            ready(n.next())
            vec.tensor_scalar(lap_ids[:, :], lap_ids[:, :], flag[:, 0:1], -1.0, ALU.mult, ALU.mult).then_inc(prep, 1)
            ready(n.next())
            vec.tensor_scalar(range_f[:, :, 2], lap_ids[:, :], 1.0, None, ALU.add).then_inc(prep, 1)
            ready(n.next())
            vec.tensor_scalar(sweeps_f[:, 0:1], flag[:, 0:1], float(TILES - 1), 1.0, ALU.mult, ALU.add).then_inc(prep, 1)
            ready(n.next())
            vec.tensor_copy(sweeps_i[:, 0:1], sweeps_f[:, 0:1]).then_inc(prep, 1)
            ready(n.next())
            vec.tensor_copy(ranges[:, :, :], range_f[:, :, :]).then_inc(prep, 1)
            ready(n.next())
            done["ranges"] = n.here
            vec.wait_ge(weights_loaded, 16 * N_WEIGHTS)
            for l in range(2):
                vec.tensor_tensor(w_pos1[:, l, :], w_pos[:, l, :], ident[:, :], ALU.add).then_inc(prep, 1)
                ready(n.next())
            vec.tensor_tensor(b_pd[:, :], cols[:, 4, :], cols[:, 5, :], ALU.add).then_inc(prep, 1)
            ready(n.next())
            vec.wait_ge(gate_exp, 1)
            vec.tensor_scalar(gate_1[:, :], gate_e[:, :], 1.0, None, ALU.add).then_inc(prep, 1)
            ready(n.next())
            vec.reciprocal(gate[:, :], gate_1[:, :]).then_inc(prep, 1)
            ready(n.next())
            done["all"] = n.here

            def degrees():
                vec.wait_ge(prep_pe, 4)
                vec.tensor_scalar(hist_src[:, :], hist_ps[:, 0:TILES], -float(n_edges) / n_nodes, None, ALU.add).then_inc(prep, 1)
                ready(n.next())
                vec.tensor_tensor(deg_dev[:, :], hist_src[:, :], valid[:, :], ALU.mult).then_inc(prep, 1)
                ready(n.next())
                vec.tensor_tensor(sq[:, :], deg_dev[:, :], deg_dev[:, :], ALU.mult).then_inc(prep, 1)
                ready(n.next())
                vec.tensor_reduce(sq_1[:, :], sq[:, :], AX_X, ALU.add).then_inc(prep, 1)
                ready(n.next())
                done["squares"] = n.here
                vec.wait_ge(prep_pe, 5)
                vec.tensor_scalar(std_f[:, 0:1], small_ps[:, 200:201], 1.0 / (n_nodes - 1), None, ALU.mult).then_inc(prep, 1)
                ready(n.next())
                r = rsqrt(std_f[:, 0:1], ready, prep, n, 1, 0.0)
                vec.tensor_scalar(std_f[:, 1:2], r, std_f[:, 0:1], 1e-6, ALU.mult, ALU.add).then_inc(prep, 1)
                ready(n.next())
                vec.reciprocal(std_f[:, 2:3], std_f[:, 1:2]).then_inc(prep, 1)
                ready(n.next())
                vec.tensor_scalar(deg_n[:, :], deg_dev[:, :], std_f[:, 2:3], None, ALU.mult).then_inc(prep, 1)
                ready(n.next())
                done["degrees"] = n.here

            sweeps = vec.value_load(sweeps_i[0:1, 0:1], min_val=1, max_val=TILES)

            def layernorm(to, v, m, signal, arrived=None):
                for i in range(TB):
                    if arrived is not None:
                        arrived(i)
                    ins = vec.bn_stats(stats[:, i, :], v(i))
                ins.then_inc(tile_step, 1)
                vec.wait_ge(tile_step, m.next())
                for i in range(TB):
                    ins = vec.bn_aggr(moments[:, i, :], stats[:, i, :])
                ins.then_inc(tile_step, 1)
                vec.wait_ge(tile_step, m.next())
                r = rsqrt(moments[:, :, 1], lambda c: vec.wait_ge(tile_step, c), tile_step, m, TB, EPS)
                for i in range(TB):
                    ins = vec.tensor_scalar(to(i), v(i), moments[:, i, 0:1], r[:, i:i + 1], ALU.subtract, ALU.mult)
                ins.then_inc(signal, 1)

            def load_shift(t):
                return vec.value_load(ranges[0:1, bass.ds(t, 1), 2:3].rearrange("a t c -> a (t c)"), min_val=-MAX_SEQ, max_val=1)

            def make_mask(to, t, g, shift_g, h):
                col = nc.s_assert_within((g + shift_g) * GC, 0, COLS,
                                         skip_runtime_bounds_check_because="the ranges end with the sweep's last group")
                return vec.scalar_tensor_tensor(
                    out=to, in0=dst_f[:, bass.ds(col + 2 * h, 2)].unsqueeze(2).broadcast_to([P, 2, P]),
                    scalar=neg_first[:, bass.ds(t, 1)], in1=lane[:, :].unsqueeze(1).broadcast_to([P, 2, P]),
                    op0=ALU.add, op1=ALU.is_equal)

            def mask_half(p, t, g, shift_g, h):
                a = visit(p - CONVS, sweeps, t, g)
                make_mask(mask_bf[:, bass.ds(a & 1, 1), 2 * h:2 * h + 2, :].rearrange("p a c n -> p (a c) n"),
                          t, g, shift_g, h).then_inc(mask_bf_ready, 1)

            def tile(p, b, i, has_next):
                t = b * TB + i
                first, last = tile_range(vec, t)
                shift_g = load_shift(t)
                conv = p < CONVS

                def masks(g):
                    v = visit(p, sweeps, t, g)
                    for h in range(2):
                        vec.wait_ge(masks_used, v * 2 + h + 1)
                        make_mask(mask[:, 2 * h:2 * h + 2, :], t, g, shift_g, h).then_inc(masks_ready, 1)

                def weigh(g, ahead):
                    a = visit(p - CONVS, sweeps, t, g)
                    slot = (g % RG) * GC
                    if ahead is not None:
                        ahead(0)
                    vec.wait_ge(group_landed, pass_base(p, sweeps) + g + 1)
                    for h in range(2):
                        vec.wait_ge(q_ready, a * 2 + h + 1)
                        vec.tensor_tensor(qk[:, 2 * h:2 * h + 2, :], q_ps[h][:, 0:2 * D].rearrange("p (c f) -> p c f", c=2),
                                          ring[:, bass.ds(slot + 2 * h, 2), 0:D], ALU.mult).then_inc(edge_step, 1)
                    vec.wait_ge(edge_step, 2)
                    vec.tensor_reduce(dots[:, :, :], qk[:, :, :].rearrange("p c (h d) -> p c h d", h=H),
                                      AX_X, ALU.add).then_inc(q_used, 1)
                    vec.wait_ge(q_used, a + 2)
                    vec.tensor_scalar(clip_a[:, :, :], dots[:, :, :], -4 * CLIP, 4 * CLIP, ALU.max, ALU.min)
                    vec.tensor_scalar(clip_b[:, :, :], dots[:, :, :], 4 * CLIP, -4 * CLIP, ALU.min, ALU.max).then_inc(edge_step, 1)
                    vec.wait_ge(edge_step, 3)
                    vec.sem_clear(edge_step)
                    vec.tensor_tensor(logits[:, :, :], clip_a[:, :, :], clip_b[:, :, :], ALU.add).then_inc(logits_ready, 1)
                    if ahead is not None:
                        ahead(1)
                    vec.wait_ge(exp_ready, a + 1)
                    vec.tensor_tensor(
                        msg[:, :, 0:D].rearrange("p c (h d) -> p c h d", h=H),
                        ring[:, bass.ds(slot, GC), D:KV].rearrange("p c (h d) -> p c h d", h=H),
                        msg[:, :, D:MSG].unsqueeze(3).broadcast_to([P, GC, H, HD]), ALU.mult).then_inc(msg_ready, 1)

                if conv:
                    with vec.If(first < last):
                        with vec.Fori(first, last) as g:
                            masks(g)
                    with vec.Else():
                        pass
                    masks(last)
                else:
                    with vec.If(first < last):
                        with vec.Fori(first, last) as g:
                            weigh(g, lambda h: mask_half(p, t, g + 1, shift_g, h))
                    with vec.Else():
                        pass
                    if has_next:
                        shift_next = load_shift(t + 1)
                        weigh(last, lambda h: mask_half(p, t + 1, last, shift_next, h))
                    else:
                        weigh(last, None)
                if p == 0:
                    onehots(1, t)
                if conv:
                    vec.wait_ge(masks_used, visit(p, sweeps, t, last) * 2 + 4)
                else:
                    vec.wait_ge(msg_used, visit(p - CONVS, sweeps, t, last) + 2)
                F = WIDTH[p]
                dinv_t = dinv[:, bass.ds(t, 1)]
                if p < 3:
                    vec.tensor_scalar(rows_a[:, bass.ds(i, 1), 0:F].rearrange("p a f -> p (a f)"), acc_ps[:, 0:F],
                                      dinv_t, None, ALU.mult).then_inc(step["acc_read"], 1)
                elif p == 3:
                    vec.scalar_tensor_tensor(out=rows_a[:, bass.ds(i, 1), 0:D].rearrange("p a f -> p (a f)"), in0=acc_ps[:, 0:D],
                                             scalar=dinv_t, in1=x_sb[:, bass.ds(t, 1), :].rearrange("p a f -> p (a f)"),
                                             op0=ALU.mult, op1=ALU.add).then_inc(step["acc_read"], 1)
                else:
                    vec.reciprocal(rden[:, :], acc_ps[:, D:MSG]).then_inc(tile_step, 1)
                    vec.wait_ge(tile_step, 1)
                    vec.sem_clear(tile_step)
                    vec.tensor_tensor(rows_a[:, bass.ds(i, 1), 0:D].rearrange("p a (h d) -> p (a h) d", h=H),
                                      acc_ps[:, 0:D].rearrange("p (h d) -> p h d", h=H),
                                      rden[:, :].unsqueeze(2).broadcast_to([P, H, HD]), ALU.mult).then_inc(step["acc_read"], 1)

            def nodes(p, b):
                m = Steps()

                def tiles_of(array, t0, t1):
                    return array[:, bass.ds(b * TB + t0, t1 - t0)]

                def settle():
                    vec.wait_ge(tile_step, m.next())

                vec.wait_ge(step["acc_read"], at("acc_read", p, b, TB) + 1)
                if p < 3:
                    def gated(i):
                        if i % 2 == 0:
                            vec.wait_ge(step["gated"], at("gated", p, b, i // 2 + 1))
                    layernorm(lambda i: rows_a[:, i, :], lambda i: rows_a[:, i, :], m, tile_step, gated)
                    settle()
                    for t0, t1 in halves:
                        vec.tensor_tensor(rows_a[:, t0:t1, :], rows_a[:, t0:t1, :],
                                          gain[:, p, :].unsqueeze(1).broadcast_to([P, t1 - t0, HID]), ALU.mult).then_inc(tile_step, 1)
                    for t0, t1 in halves:
                        settle()
                        vec.tensor_tensor(rows_a[:, t0:t1, :], rows_a[:, t0:t1, :],
                                          shift[:, p, :].unsqueeze(1).broadcast_to([P, t1 - t0, HID]), ALU.add).then_inc(step["normed"], 1)
                    for h, (t0, t1) in enumerate(halves):
                        vec.wait_ge(step["elu_parts"], at("elu_parts", p, b, h + 1))
                        vec.scalar_tensor_tensor(out=rows_a[:, t0:t1, :], in0=rows_a[:, t0:t1, :], scalar=0.0, in1=exp_part[:, t0:t1, :],
                                                 op0=ALU.max, op1=ALU.add).then_inc(tile_step, 1)
                        settle()
                        if p < 2:
                            ins = vec.scalar_tensor_tensor(out=tiles_of(own, t0, t1), in0=rows_a[:, t0:t1, :], scalar=-1.0,
                                                           in1=tiles_of(dinv, t0, t1).unsqueeze(2).broadcast_to([P, t1 - t0, HID]),
                                                           op0=ALU.add, op1=ALU.mult)
                        else:
                            ins = vec.tensor_scalar(rows_a[:, t0:t1, :], rows_a[:, t0:t1, :], -1.0, None, ALU.add)
                    if p < 2:
                        ins.then_inc(step["nodes_done"], 1)
                        return
                    ins.then_inc(step["hidden_ready"], 1)
                    for u, (t0, t1) in enumerate(fours):
                        vec.wait_ge(step["last_mixed"], at("last_mixed", p, b, u + 1))
                        ins = vec.tensor_tensor(tiles_of(own, t0, t1)[:, :, 0:D],
                                                banks[2 + u][:, 0:(t1 - t0) * D].rearrange("p (t f) -> p t f", f=D),
                                                tiles_of(dinv, t0, t1).unsqueeze(2).broadcast_to([P, t1 - t0, D]), ALU.mult)
                    ins.then_inc(step["nodes_done"], 1)
                    return

                sums = rows_a[:, :, 0:D]
                z = rows_a[:, :, D:2 * D]

                def x_t(i):
                    return x_sb[:, bass.ds(b * TB + i, 1), :].rearrange("p a f -> p (a f)")

                def lx_t(i):
                    return layer_x[:, bass.ds(b * TB + i, 1), :].rearrange("p a f -> p (a f)")

                def project():
                    vec.tensor_tensor(deg_diag[:, :, :], ident[:, :].unsqueeze(1).broadcast_to([P, TB, P]),
                                      tiles_of(deg_n, 0, TB).unsqueeze(2).broadcast_to([P, TB, P]), ALU.mult).then_inc(step["xn_ready"], 1)
                    vec.wait_ge(step["qkv_copied"], at("qkv_copied", p, b, TB))
                    vec.tensor_tensor(own_qk[:, :, :], tiles_of(q_rows, 0, TB), kv_new[:, :, 0:D], ALU.mult).then_inc(tile_step, 1)
                    settle()
                    vec.tensor_reduce(own_dots[:, :, :], own_qk[:, :, :].rearrange("p t (h d) -> p t h d", h=H), AX_X, ALU.add).then_inc(tile_step, 1)
                    settle()
                    vec.tensor_scalar(own_a[:, :, :], own_dots[:, :, :], -4 * CLIP, 4 * CLIP, ALU.max, ALU.min)
                    vec.tensor_scalar(own_b[:, :, :], own_dots[:, :, :], 4 * CLIP, -4 * CLIP, ALU.min, ALU.max).then_inc(tile_step, 1)
                    settle()
                    vec.tensor_tensor(own_logits[:, :, :], own_a[:, :, :], own_b[:, :, :], ALU.add).then_inc(step["self_logits"], 1)
                    vec.wait_ge(step["self_exp"], at("self_exp", p, b, 1))
                    vec.tensor_tensor(tiles_of(own_msg, 0, TB)[:, :, 0:D].rearrange("p t (h d) -> p t h d", h=H),
                                      kv_new[:, :, D:KV].rearrange("p t (h d) -> p t h d", h=H),
                                      tiles_of(own_msg, 0, TB)[:, :, D:MSG].unsqueeze(3).broadcast_to([P, TB, H, HD]),
                                      ALU.mult).then_inc(step["nodes_done"], 1)

                if p == 3:
                    vec.tensor_tensor(sums, sums, b3_all[:, :].unsqueeze(1).broadcast_to([P, TB, D]), ALU.add).then_inc(tile_step, 1)
                    settle()
                    layernorm(x_t, lambda i: sums[:, i, :], m, tile_step)
                    settle()
                    layernorm(lambda i: sums[:, i, :], x_t, m, tile_step)
                    m.next()
                    project()
                    return

                for u, (t0, t1) in enumerate(fours):
                    vec.wait_ge(step["attended"], at("attended", p, b, u + 1))
                    ins = vec.tensor_tensor(z[:, t0:t1, :], banks[2 + u][:, 0:(t1 - t0) * D].rearrange("p (t f) -> p t f", f=D),
                                            tiles_of(x_sb if p == CONVS else layer_x, t0, t1), ALU.add)
                ins.then_inc(tile_step, 1)
                settle()
                layernorm(lambda i: sums[:, i, :], lambda i: z[:, i, :], m, step["z_ready"])
                for u, (t0, t1) in enumerate(fours):
                    vec.wait_ge(step["ff_out"], at("ff_out", p, b, u + 1))
                    ins = vec.tensor_tensor(tiles_of(layer_x, t0, t1) if p == CONVS else z[:, t0:t1, :],
                                            banks[u][:, 0:(t1 - t0) * D].rearrange("p (t f) -> p t f", f=D), z[:, t0:t1, :], ALU.add)
                ins.then_inc(tile_step, 1)
                settle()
                if p == CONVS:
                    layernorm(lambda i: sums[:, i, :], lx_t, m, tile_step)
                    m.next()
                    project()
                else:
                    vec.tensor_tensor(z[:, :, :], z[:, :, :], tiles_of(x_sb, 0, TB), ALU.add).then_inc(tile_step, 1)
                    settle()
                    layernorm(lx_t, lambda i: z[:, i, :], m, step["nodes_done"])

            for p in range(PASSES):
                with vec.Fori(0, NB) as b:
                    if p < CONVS:
                        with vec.Fori(0, TB) as i:
                            tile(p, b, i, True)
                    else:
                        first, _ = tile_range(vec, b * TB)
                        shift_g = load_shift(b * TB)
                        for h in range(2):
                            mask_half(p, b * TB, first, shift_g, h)
                        with vec.Fori(0, TB - 1) as i:
                            tile(p, b, i, True)
                        tile(p, b, TB - 1, False)
                    nodes(p, b)
                    vec.wait_ge(step["nodes_done"], at("nodes_done", p, b, 1))
                    vec.sem_inc(batch_seen, 1)
                    vec.sem_clear(tile_step)
                if p == 0:
                    degrees()

        @block.sync
        def _(sp):
            sp.dma_start(here[:, :], w["dst_rows"]).then_inc(loaded, 16)
            sp.wait_ge(consts_ready, 1)
            flat = w["dst_flat"]
            sp.dma_start(dst_i[:, 0:MAIN], w["dst_main"]).then_inc(loaded, 16)
            sp.dma_start(dst_i[0:TAIL, MAIN:MAIN + 1], w["dst_tail"]).then_inc(loaded, 16)
            sp.dma_start(ids[:, 0:MAIN], w["src_main"]).then_inc(loaded, 16)
            sp.dma_start(ids[0:TAIL, MAIN:MAIN + 1], w["src_tail"]).then_inc(loaded, 16)
            k = (in_rows - 1) * in_cols
            sp.dma_start(after[0:in_rows - 1, :], flat[1:1 + k].rearrange("(r c) -> r c", c=in_cols)).then_inc(loaded, 16)
            sp.dma_start(after[in_rows - 1:in_rows, 0:in_cols - 1], flat[1 + k:n_edges].rearrange("(r c) -> r c", r=1)).then_inc(loaded, 16)
            sp.dma_start(x_sb[:, 0:TILES - 1, :], w["x"][0:(TILES - 1) * P, :].rearrange("(t p) f -> p t f", p=P)).then_inc(loaded, 16)
            sp.dma_start(x_sb[0:LAST_ROWS, TILES - 1, :], w["x"][(TILES - 1) * P:n_nodes, :]).then_inc(loaded, 16)
            sp.dma_start(gate_in[:, :], w["gates"].rearrange("(a n) -> a n", a=1).broadcast_to([P, 3])).then_inc(loaded, 16)

            def load(to, src):
                sp.dma_start(to, src).then_inc(weights_loaded, 16)
            for l in range(4):
                load(conv_w[l][:, :, :], w[f"L0_gnn_W{l}"].rearrange("(k p) n -> p k n", p=P))
            row = "(a n) -> a n"
            for l in range(3):
                load(conv_b[l], w[f"L0_gnn_b{l}"].rearrange(row, a=1))
                load(gain[:, l, :], w[f"L0_gnn_g{l}"].rearrange(row, a=1).broadcast_to([P, HID]))
                load(shift[:, l, :], w[f"L0_gnn_beta{l}"].rearrange(row, a=1).broadcast_to([P, HID]))
            load(b3_all[:, :], w["L0_gnn_b3"].rearrange(row, a=1).broadcast_to([P, D]))
            for l in range(2):
                for i, m in enumerate(("Wq", "Wk", "Wv")):
                    load(w_qkv[:, l, i * D:(i + 1) * D], w[f"L1_gnn_{m}"][l, :, :])
                for i, m in enumerate(("bq", "bk", "bv")):
                    load(b_qkv[:, l, i * D:(i + 1) * D], w[f"L1_gnn_{m}"][l:l + 1, :])
                load(w_ff2[:, l, :, :], w["L1_gnn_W2"][l, :, :].rearrange("(c p) n -> p c n", p=P))
                load(w_o[:, l, :], w["L1_gnn_Wo"][l, :, :])
                load(w_ff1[:, l, :], w["L1_gnn_W1"][l, :, :])
                load(w_pos[:, l, :], w["L1_gnn_Wpos"][l, :, :])
                load(w_deg[:, l, :], w["L1_gnn_Wdeg"][l, :, :].broadcast_to([P, D]))
                load(b_o[:, l, :], w["L1_gnn_bo"][l:l + 1, :])
                load(b_ff2[:, l, :], w["L1_gnn_b2"][l:l + 1, :])
            load(cols[:, :, :], w["layer_cols"])
            load(b_ff1[:, :, :], w["ff1_cols"])
            sp.wait_ge(prep, done["ranges"])
            sweeps = sp.value_load(sweeps_i[0:1, 0:1], min_val=1, max_val=TILES)
            for p in range(PASSES):
                with sp.Fori(0, sweeps) as s:
                    with sp.Fori(0, LAPS) as lap:
                        count = (p * sweeps + s) * LAPS + lap + 1
                        for q in range(RG):
                            for j in range(q * GC, (q + 1) * GC):
                                sp.wait_ge(landed[j], count * 16)
                            sp.sem_inc(group_landed, 1)
            OUTPUTS = NB * (1 + (TB > 1))
            if NB > 1 and LAST_ROWS < P:
                sp.wait_ge(step["nodes_done"], at("nodes_done", PASSES - 1, NB - 1, 1))
                for b in range(NB - 1):
                    t = b * TB + TB - 1
                    sp.dma_start(out[t * P + LAST_ROWS:(t + 1) * P, :], layer_x[LAST_ROWS:P, t, :]).then_inc(out_written, 16)
                OUTPUTS += NB - 1
            sp.wait_ge(out_written, 16 * OUTPUTS)
            sp.wait_ge(rows_written, 16 * (NB * (PASSES - 1) + 1))

        @block.gpsimd
        def _(pool):
            pool.memset(dst_i[:, :], -1)
            pool.memset(ids[:, :], -1)
            pool.memset(after[:, :], 1 << 30)
            pool.memset(x_sb[:, TILES - 1, :], 0.0)
            pool.drain().then_inc(consts_ready, 1)
            exact = dict(allow_small_or_imprecise_dtypes=True)
            pool.iota(lane[:, :], [[1, P]], base=0, channel_multiplier=0, **exact)
            pool.iota(lane_bf[:, :], [[1, P]], base=0, channel_multiplier=0, **exact)
            pool.iota(part[:, :], [[0, 1]], base=0, channel_multiplier=1, **exact)
            pool.iota(node_id[:, :], [[P, TILES]], base=0, channel_multiplier=1, **exact)
            pool.iota(neg_first[:, :], [[-P, TILES]], base=0, channel_multiplier=0, **exact)
            pool.iota(lane_t[:, :], [[1, TILES + 1]], base=0, channel_multiplier=0, **exact)
            pool.iota(unsorted_start[:, :], [[GROUPS, TILES + 1]], base=-1, channel_multiplier=0, **exact)
            pool.iota(lap_ids[:, :], [[GROUPS, TILES + 1]], base=0, channel_multiplier=0, **exact)
            pool.memset(ones[:, :], 1.0)
            pool.memset(zeros_bf[:, :], 0.0)
            pool.memset(range_f[:, :, :], 0.0)
            pool.drain().then_inc(consts_ready, 1)

            pool.wait_ge(prep, done["ranges"])
            sweeps = pool.value_load(sweeps_i[0:1, 0:1], min_val=1, max_val=TILES)
            pool.tensor_copy(idx_stage[:, 0, :], src_idx[:, 0:RING]).then_inc(idx_staged, 1)
            for p in range(PASSES):
                pool.wait_ge(rows_written, 16 * (NB * p + 1))
                if p > 0:
                    pool.sem_inc(groups_freed, 1)
                with pool.Fori(0, sweeps) as s:
                    with pool.Fori(0, LAPS // 2) as two:
                        for half in range(2):
                            n = p * (LAPS * sweeps) + s * LAPS + two * 2 + half
                            for q in range(RG):
                                if q == 0:
                                    pool.wait_ge(idx_staged, n + 1)
                                    pool.sem_inc(staging_seen, 1)
                                pool.wait_ge(groups_freed, n * RG + q + 1)
                                pool.sem_inc(slots_seen, 1)
                                for j in range(q * GC, (q + 1) * GC):
                                    pool.indirect_dma_start(
                                        ring[:, j, 0:WIDTH[p]], None, tables[p][:, :],
                                        bass.IndirectOffsetOnAxis(ap=idx_stage[:, half, j:j + 1], axis=0),
                                    ).then_inc(landed[j], 16)
                                if q == RG // 2:
                                    pool.wait_ge(group_landed, n * RG + 1)
                                    pool.sem_inc(staging_seen, 1)
                                    pool.tensor_copy(idx_stage[:, 1 - half, :],
                                                     src_idx[:, bass.ds((two * 2 + half + 1) * RING, RING)]).then_inc(idx_staged, 1)

        @block.scalar
        def _(act):
            act.wait_ge(loaded, 16 * LOADS_IN)
            act.activation(gate_e[:, :], gate_in[:, :], ACT.Exp, scale=-1.0).then_inc(gate_exp, 1)
            act.wait_ge(prep, done["rows"])
            act.dma_start(tables[0].rearrange("(t p) f -> p t f", p=P), own[:, :, 0:D]).then_inc(rows_written, 16)
            act.wait_ge(prep, done["all"])
            sweeps = act.value_load(sweeps_i[0:1, 0:1], min_val=1, max_val=TILES)

            def turned_half(a, h):
                act.wait_ge(masks_turned, a * 2 + h + 1)
                act.activation(mask_t[:, 2 * h:2 * h + 2, :], maskt_ps[h][:, 0:2 * P].rearrange("p (c n) -> p c n", c=2),
                               ACT.Copy).then_inc(mask_t_ready, 1)

            def tile(p, b, i, has_next):
                t = b * TB + i
                first, last = tile_range(act, t)

                if p < CONVS:
                    with act.If(first < last):
                        with act.Fori(first, last) as g:
                            act.wait_ge(masks_used, visit(p, sweeps, t, g) * 2 + 4)
                            act.sem_inc(groups_freed, 1)
                    with act.Else():
                        pass
                    return

                def group(g, freed, ahead):
                    a = visit(p - CONVS, sweeps, t, g)
                    if ahead:
                        turned_half(a + 1, 0)
                    act.wait_ge(msg_used, a + 1)
                    act.sem_inc(keep_seen, 1)
                    act.activation(mask[:, :, :], mask_bf[:, bass.ds(a & 1, 1), :, :].rearrange("p a c n -> p (a c) n"),
                                   ACT.Copy).then_inc(mask_kept, 1)
                    act.wait_ge(logits_ready, a + 1)
                    act.activation(msg[:, :, D:MSG], logits[:, :, :], ACT.Exp, scale=0.5 / HD ** 0.5).then_inc(exp_ready, 1)
                    if ahead:
                        turned_half(a + 1, 1)
                    if freed:
                        act.wait_ge(msg_ready, a + 1)
                        act.sem_inc(groups_freed, 1)

                with act.If(first < last):
                    with act.Fori(first, last) as g:
                        group(g, True, True)
                with act.Else():
                    pass
                group(last, False, has_next)

            def nodes(p, b):
                def columns(units, width, k0, scale=1.0, bias=None):
                    K = width // P
                    for u, (t0, t1) in enumerate(units):
                        act.wait_ge(step["turned"], at("turned", p, b, k0 + u + 1))
                        to = (conv_t if p < 3 else turn_b)[:, t0 * K:t1 * K, :]
                        v = banks[u % 2][:, 0:(t1 - t0) * width].rearrange("p (t n) -> p t n", n=P)
                        if bias is None:
                            ins = act.activation(to, v, ACT.Copy)
                        else:
                            ins = act.activation(to, v, ACT.Identity, scale=scale, bias=bias)
                        ins.then_inc(step["columns"], 1)

                def project(l, k0):
                    columns(fours, D, k0, cols[:, 0, l:l + 1], cols[:, 1, l:l + 1])
                    for u, (t0, t1) in enumerate(fours):
                        act.wait_ge(step["pos_mixed"], at("pos_mixed", p, b, u + 1))
                        act.activation(xp_t[:, t0:t1, :], banks[2 + u][:, 0:(t1 - t0) * P].rearrange("p (t n) -> p t n", n=P),
                                       ACT.Identity, bias=b_pd[:, l:l + 1]).then_inc(step["xp_columns"], 1)
                    for i in range(TB):
                        act.wait_ge(step["qkv_mixed"], at("qkv_mixed", p, b, i + 1))
                        qkv = banks[4 + i % 3]
                        act.activation(q_rows[:, bass.ds(b * TB + i, 1), :].rearrange("p a f -> p (a f)"), qkv[:, 0:D], ACT.Copy)
                        act.activation(kv_new[:, i, :], qkv[:, D:3 * D], ACT.Copy).then_inc(step["qkv_copied"], 1)
                    act.wait_ge(step["qkv_copied"], at("qkv_copied", p, b, TB))
                    act.dma_start(tables[p + 1][bass.ds(b * (TB * P), TB * P), :].rearrange("(t p) f -> p t f", p=P),
                                  kv_new[:, :, :]).then_inc(rows_written, 16)
                    act.wait_ge(step["self_logits"], at("self_logits", p, b, 1))
                    act.activation(own_msg[:, bass.ds(b * TB, TB), D:MSG], own_logits[:, :, :], ACT.Exp,
                                   scale=0.5 / HD ** 0.5).then_inc(step["self_exp"], 1)

                act.wait_ge(rows_written, 16 * (NB * p + 1 + (b if p < PASSES - 1 else 0)))
                if p < 3:
                    columns(pairs, WIDTH[p], 0)
                    for u, (t0, t1) in enumerate(pairs):
                        act.wait_ge(step["mixed"], at("mixed", p, b, u + 1))
                        act.activation(rows_a[:, t0:t1, :], banks[2 + u][:, 0:(t1 - t0) * HID].rearrange("p (t f) -> p t f", f=HID),
                                       ACT.Identity, scale=gate[:, p:p + 1]).then_inc(step["gated"], 1)
                    for h, (t0, t1) in enumerate(halves):
                        act.wait_ge(step["normed"], at("normed", p, b, h + 1))
                        act.activation(exp_part[:, t0:t1, :], rows_a[:, t0:t1, :], ACT.Relu, scale=-1.0).then_inc(step["elu_neg"], 1)
                        act.wait_ge(step["elu_neg"], at("elu_neg", p, b, h + 1))
                        act.activation(exp_part[:, t0:t1, :], exp_part[:, t0:t1, :], ACT.Exp, scale=-1.0).then_inc(step["elu_parts"], 1)
                    if p == 2:
                        columns(pairs, HID, U2)
                    act.wait_ge(step["nodes_done"], at("nodes_done", p, b, 1))
                    act.dma_start(tables[p + 1][bass.ds(b * (TB * P), TB * P), :].rearrange("(t p) f -> p t f", p=P),
                                  own[:, bass.ds(b * TB, TB), 0:WIDTH[p + 1]]).then_inc(rows_written, 16)
                    return
                if p == 3:
                    project(0, 0)
                    return
                l = p - CONVS
                columns(fours, D, 0)
                columns(fours, D, U4, cols[:, 2, l:l + 1], cols[:, 3, l:l + 1])
                for u, (t0, t1) in enumerate(fours):
                    for c in range(FC):
                        act.wait_ge(step["ff_mixed"], at("ff_mixed", p, b, u * FC + c + 1))
                        act.activation(ff_t[:, c, t0 * P:t1 * P], banks[2 + c][:, 0:(t1 - t0) * P], ACT.Gelu,
                                       bias=b_ff1[:, l, c:c + 1]).then_inc(step["ff_gelu"], 1)
                if l == 0:
                    project(1, 2 * U4)
                    return
                act.wait_ge(step["nodes_done"], at("nodes_done", p, b, 1))
                if TB > 1:
                    act.dma_start(out[bass.ds(b * (TB * P), (TB - 1) * P), :].rearrange("(t p) f -> p t f", p=P),
                                  layer_x[:, bass.ds(b * TB, TB - 1), :]).then_inc(out_written, 16)
                act.dma_start(out[bass.ds(b * (TB * P) + (TB - 1) * P, LAST_ROWS), :],
                              layer_x[0:LAST_ROWS, bass.ds(b * TB + TB - 1, 1), :].rearrange("p a f -> p (a f)")).then_inc(out_written, 16)

            for p in range(PASSES):
                with act.Fori(0, NB) as b:
                    if p < CONVS:
                        with act.Fori(0, TB) as i:
                            tile(p, b, i, True)
                    else:
                        act.activation(warm[:, :], part[:, :], ACT.Exp, scale=-1.0)
                        first, _ = tile_range(act, b * TB)
                        for h in range(2):
                            turned_half(visit(p - CONVS, sweeps, b * TB, first), h)
                        with act.Fori(0, TB - 1) as i:
                            tile(p, b, i, True)
                        tile(p, b, TB - 1, False)
                    nodes(p, b)

        @block.tensor
        def _(pe):
            pe.sem_inc(onehots_used, 2)
            pe.sem_inc(masks_used, 2)
            pe.sem_inc(q_used, 1)
            pe.sem_inc(msg_used, 1)
            pe.sem_inc(groups_freed, RG)
            pe.sem_inc(step["acc_read"], 1)
            pe.wait_ge(consts_ready, 2)

            def count_open():
                pe.matmul(hist_ps[:, 0:TILES], zeros_bf[:, :], zeros_bf[:, 0:TILES], start=True, stop=False)

            def count(e, b):
                for h, (j0, j1) in enumerate([(0, HC // 2), (HC // 2, HC)]):
                    pe.wait_ge(onehots_ready, (TILES * e + b) * 2 + h + 1)
                    for j in range(j0, j1):
                        ins = pe.matmul(hist_ps[:, 0:TILES], one_lo[:, j, :], one_hi[:, j, :], start=False, stop=False)
                    ins.then_inc(onehots_used, 1)

            def count_close():
                pe.matmul(hist_ps[:, 0:TILES], zeros_bf[:, :], zeros_bf[:, 0:TILES], start=False, stop=True).then_inc(prep_pe, 1)

            count_open()
            with pe.Fori(0, TILES) as b:
                count(0, b)
            count_close()
            pe.wait_ge(prep, done["falls"])
            pe.matmul(small_ps[0:1, 0:1], falls_1[:, :], ones[0:in_rows, 0:1], start=True, stop=True)
            pe.matmul(small_ps[0:TILES, 1:2], hist[:, :], ones[:, 0:1], start=True, stop=True).then_inc(prep_pe, 1)
            pe.wait_ge(prep, done["counts"])
            pe.matmul(small_ps[0:1, 64:64 + TILES + 1], count_col[:, :], tri[:, :], start=True, stop=True).then_inc(prep_pe, 1)
            pe.wait_ge(prep, done["all"])
            sweeps = pe.value_load(sweeps_i[0:1, 0:1], min_val=1, max_val=TILES)

            def turn(to, v):
                return pe.matmul(to, v, ident[:, :], start=True, stop=True)

            def spread_q(p, t, g):
                a = visit(p - CONVS, sweeps, t, g)
                q_t = q_rows[:, bass.ds(t, 1), :].rearrange("p a f -> p (a f)")
                for h in range(2):
                    pe.wait_ge(mask_bf_ready, a * 2 + h + 1)
                    for j in (2 * h, 2 * h + 1):
                        ins = pe.matmul(maskt_ps[h][:, (j % 2) * P:(j % 2 + 1) * P],
                                        mask_bf[:, bass.ds(a & 1, 1), j, :].rearrange("p a n -> p (a n)"), ident_bf[:, :], start=True, stop=True)
                    ins.then_inc(masks_turned, 1)
                    if h == 0:
                        pe.wait_ge(q_used, a + 1)
                    pe.wait_ge(mask_t_ready, a * 2 + h + 1)
                    for j in (2 * h, 2 * h + 1):
                        ins = pe.matmul(q_ps[h][:, (j % 2) * D:(j % 2 + 1) * D], mask_t[:, j, :], q_t, start=True, stop=True)
                    ins.then_inc(q_ready, 1)

            def tile(p, b, i, has_next):
                t = b * TB + i
                first, last = tile_range(pe, t)
                conv = p < CONVS
                F = WIDTH[p] if conv else MSG
                pe.wait_ge(step["acc_read"], at("acc_read", p, b, i) + 1)
                mine = own[:, bass.ds(t, 1), 0:F] if conv else own_msg[:, bass.ds(t, 1), :]
                pe.matmul(acc_ps[:, 0:F], ident[:, :], mine.rearrange("p a f -> p (a f)"), start=True, stop=False)

                def group(g, final):
                    v = visit(p, sweeps, t, g)
                    slot = (g % RG) * GC
                    if conv:
                        pe.wait_ge(group_landed, pass_base(p, sweeps) + g + 1)
                    else:
                        a = visit(p - CONVS, sweeps, t, g)
                        pe.wait_ge(mask_kept, a + 1)
                        pe.wait_ge(msg_ready, a + 1)
                    for h in range(2):
                        if conv:
                            pe.wait_ge(masks_ready, v * 2 + h + 1)
                        for j in (2 * h, 2 * h + 1):
                            rhs = ring[:, bass.ds(slot + j, 1), 0:F].rearrange("p a f -> p (a f)") if conv else msg[:, j, :]
                            ins = pe.matmul(acc_ps[:, 0:F], mask[:, j, :], rhs, start=False, stop=final and j == GC - 1)
                        if conv:
                            ins.then_inc(masks_used, 1)
                    if not conv:
                        ins.then_inc(msg_used, 1)

                with pe.If(first < last):
                    with pe.Fori(first, last) as g:
                        if not conv:
                            spread_q(p, t, g + 1)
                        group(g, False)
                with pe.Else():
                    pass
                if not conv and has_next:
                    spread_q(p, t + 1, last)
                group(last, True)
                if p == 0:
                    count(1, t)

            def nodes(p, b):
                def turn_all(v, units, width, k0):
                    for u, (t0, t1) in enumerate(units):
                        if u >= 2:
                            pe.wait_ge(step["columns"], at("columns", p, b, k0 + u - 1))
                        for t in range(t0, t1):
                            for k in range(width // P):
                                c = (t - t0) * width + k * P
                                ins = turn(banks[u % 2][:, c:c + P], v[:, t, k * P:(k + 1) * P])
                        ins.then_inc(step["turned"], 1)

                def product(bank, width, t0, t1, rows_t, weights, bias, at_row=0):
                    K = len(weights)
                    for t in range(t0, t1):
                        to = bank[:, (t - t0) * width:(t - t0 + 1) * width]
                        for k in range(K):
                            ins = pe.matmul(to, rows_t[:, t * K + k, :], weights[k], start=k == 0, stop=bias is None and k == K - 1)
                        if bias is not None:
                            ins = pe.matmul(to, ones[at_row:at_row + 1, :], bias, start=False, stop=True)
                    return ins

                def project(l, k0):
                    pe.wait_ge(step["xn_ready"], at("xn_ready", p, b, 1))
                    turn_all(rows_a[:, :, 0:D], fours, D, k0)
                    for u, (t0, t1) in enumerate(fours):
                        pe.wait_ge(step["columns"], at("columns", p, b, k0 + u + 1))
                        pos = banks[2 + u][:, 0:(t1 - t0) * P]
                        pe.matmul(pos, w_pos1[:, l, :], turn_b[:, t0:t1, :], start=True, stop=False)
                        pe.matmul(pos, w_deg[:, l, :], deg_diag[:, t0:t1, :], start=False, stop=True).then_inc(step["pos_mixed"], 1)
                    for i in range(TB):
                        if i % 4 == 0:
                            pe.wait_ge(step["xp_columns"], at("xp_columns", p, b, i // 4 + 1))
                        if i >= 3:
                            pe.wait_ge(step["qkv_copied"], at("qkv_copied", p, b, i - 2))
                        qkv = banks[4 + i % 3][:, 0:3 * D]
                        pe.matmul(qkv, xp_t[:, i, :], w_qkv[:, l, :], start=True, stop=False)
                        pe.matmul(qkv, ones[0:1, :], b_qkv[:, l, :], start=False, stop=True).then_inc(step["qkv_mixed"], 1)

                if p == 3:
                    project(0, 0)
                    return
                pe.wait_ge(step["acc_read"], at("acc_read", p, b, TB) + 1)
                if p < 3:
                    F = WIDTH[p]
                    turn_all(rows_a, pairs, F, 0)
                    for u, (t0, t1) in enumerate(pairs):
                        pe.wait_ge(step["columns"], at("columns", p, b, u + 1))
                        product(banks[2 + u], HID, t0, t1, conv_t, [conv_w[p][:, k, :] for k in range(F // P)],
                                conv_b[p], 32).then_inc(step["mixed"], 1)
                    if p == 2:
                        pe.wait_ge(step["hidden_ready"], at("hidden_ready", p, b, 1))
                        turn_all(rows_a, pairs, HID, U2)
                        for u, (t0, t1) in enumerate(fours):
                            pe.wait_ge(step["columns"], at("columns", p, b, min(2 * U2, U2 + 2 * u + 2)))
                            product(banks[2 + u], D, t0, t1, conv_t, [conv_w[3][:, k, :] for k in range(2)], None).then_inc(step["last_mixed"], 1)
                    return
                l = p - CONVS
                turn_all(rows_a, fours, D, 0)
                for u, (t0, t1) in enumerate(fours):
                    pe.wait_ge(step["columns"], at("columns", p, b, u + 1))
                    product(banks[2 + u], D, t0, t1, turn_b, [w_o[:, l, :]], b_o[:, l, :], 64).then_inc(step["attended"], 1)
                pe.wait_ge(step["z_ready"], at("z_ready", p, b, 1))
                turn_all(rows_a, fours, D, U4)
                for u, (t0, t1) in enumerate(fours):
                    pe.wait_ge(step["columns"], at("columns", p, b, U4 + u + 1))
                    for c in range(FC):
                        if u > 0:
                            pe.wait_ge(step["ff_gelu"], at("ff_gelu", p, b, (u - 1) * FC + c + 1))
                        pe.matmul(banks[2 + c][:, 0:(t1 - t0) * P], w_ff1[:, l, c * P:(c + 1) * P], turn_b[:, t0:t1, :],
                                  start=True, stop=True).then_inc(step["ff_mixed"], 1)
                for u, (t0, t1) in enumerate(fours):
                    pe.wait_ge(step["ff_gelu"], at("ff_gelu", p, b, (u + 1) * FC))
                    for t in range(t0, t1):
                        to = banks[u][:, (t - t0) * D:(t - t0 + 1) * D]
                        for c in range(FC):
                            pe.matmul(to, ff_t[:, c, t * P:(t + 1) * P], w_ff2[:, l, c, :], start=c == 0, stop=False)
                        ins = pe.matmul(to, ones[64:65, :], b_ff2[:, l, :], start=False, stop=True)
                    ins.then_inc(step["ff_out"], 1)
                if l == 0:
                    project(1, 2 * U4)

            count_open()
            for p in range(PASSES):
                pe.wait_ge(rows_written, 16 * (NB * p + 1))
                with pe.Fori(0, NB) as b:
                    if p > 0:
                        pe.wait_ge(step["nodes_done"], at("nodes_done", p, b, 0))
                        pe.sem_inc(banks_seen, 1)
                    if p < CONVS:
                        with pe.Fori(0, TB) as i:
                            tile(p, b, i, True)
                    else:
                        first, _ = tile_range(pe, b * TB)
                        spread_q(p, b * TB, first)
                        with pe.Fori(0, TB - 1) as i:
                            tile(p, b, i, True)
                        tile(p, b, TB - 1, False)
                    nodes(p, b)
                if p == 0:
                    count_close()
                    pe.wait_ge(prep, done["squares"])
                    pe.matmul(small_ps[:, 200:201], ones[:, :], sq_1[:, :], start=True, stop=True).then_inc(prep_pe, 1)


def kernel(**inputs):
    import numpy as np
    import concourse.bacc as bacc
    from concourse.bass_utils import run_bass_kernel_spmd

    a = {k: np.ascontiguousarray(v) for k, v in inputs.items()}
    n_nodes, n_edges = a["x"].shape[0], a["src"].shape[0]
    main = n_edges // P
    w = {k: v for k, v in a.items() if k not in ("src", "dst") and not k.startswith("L0_gnn_a")}
    for k in ("src", "dst"):
        w[k + "_main"] = np.ascontiguousarray(a[k][:main * P].reshape(main, P).T)
        w[k + "_tail"] = np.ascontiguousarray(a[k][main * P:].reshape(-1, 1))
    rows = max(r for r in range(1, P + 1) if n_edges % r == 0)
    w["dst_rows"] = a["dst"].reshape(rows, n_edges // rows)
    w["dst_flat"] = a["dst"]
    w["gates"] = np.concatenate([a[f"L0_gnn_a{i}"] for i in range(3)])
    w["layer_cols"] = np.ascontiguousarray(np.stack([a[f"L1_gnn_{k}"] for k in ("ln1_g", "ln1_b", "ln2_g", "ln2_b", "bpos", "bdeg")]).transpose(2, 0, 1))
    w["ff1_cols"] = np.ascontiguousarray(a["L1_gnn_b1"].reshape(2, FC, P).transpose(2, 0, 1))

    nc = bacc.Bacc("TRN2", target_bir_lowering=False, num_devices=1)
    arrays, args = {}, {}
    for k, v in w.items():
        arrays["in_" + k] = v
        args[k] = nc.dram_tensor("in_" + k, v.shape, mybir.dt.from_np(v.dtype), kind="ExternalInput").ap()
    out = nc.dram_tensor("out_0", (n_nodes, D), F32, kind="ExternalOutput").ap()
    build_gnn(nc, args, out)
    r = run_bass_kernel_spmd(nc, [arrays], core_ids=[0])
    return r.results[0]["out_0"]
```
